# Optimizing a Trainium2 kernel written in Bass

```python
import numpy as np
import jax
import jax.numpy as jnp

def _softmax(x, axis=-1):
    return jax.nn.softmax(x, axis=axis)

def _gelu(x):
    return jax.nn.gelu(x, approximate=True)

def _silu(x):
    return jax.nn.silu(x)

def _sigmoid(x):
    return jax.nn.sigmoid(x)

def _layernorm(x, axis=-1, eps=1e-05):
    m = jnp.mean(x, axis=axis, keepdims=True)
    v = jnp.var(x, axis=axis, keepdims=True)
    return (x - m) / jnp.sqrt(v + eps)

def _scatter_add(tgt, idx, src, axis=0):
    return tgt.at[idx].add(src)

def _segment_sum(src, seg, n):
    return jax.ops.segment_sum(src, seg, n)
kernel_name = 'mk_cond_resid_d4_seqx_r4_0424c8'

def setup_inputs(seed: int=0):
    np.random.seed(seed)
    _w = jnp.asarray

    def _rec_inputs():
        import jax
        import jax.numpy as jnp
        _rk = jax.random.key(seed)
        x = -0.0003929 + 0.9999 * jax.random.normal(jax.random.fold_in(_rk, 1), (8, 512, 256), jnp.float32)
        _lenS = 512 - jax.random.randint(jax.random.fold_in(_rk, 7), (8,), 0, max(1, 512 // 4) + 1, jnp.int32)
        _lenS2 = 512 - jax.random.randint(jax.random.fold_in(_rk, 8), (8,), 0, max(1, 512 // 4) + 1, jnp.int32)
        itok_B_0_2 = jax.random.randint(jax.random.fold_in(_rk, 11), (8,), 0, 3, jnp.int32)
        itok_B_0_30 = jax.random.randint(jax.random.fold_in(_rk, 12), (8,), 0, 31, jnp.int32)
        itok_B_0_7 = jax.random.randint(jax.random.fold_in(_rk, 13), (8,), 0, 8, jnp.int32)
        condB_zX = jax.random.uniform(jax.random.fold_in(_rk, 14), (8,), jnp.float32, 0.0, 0.983423)
        condB_zY = jax.random.uniform(jax.random.fold_in(_rk, 15), (8,), jnp.float32, 0.0, 0.979075)
        condB_zR = jax.random.uniform(jax.random.fold_in(_rk, 16), (8,), jnp.float32, 0.0, 0.9968)
        return (x, itok_B_0_2, itok_B_0_30, itok_B_0_7, condB_zX, condB_zY, condB_zR)
    x, itok_B_0_2, itok_B_0_30, itok_B_0_7, condB_zX, condB_zY, condB_zR = _rec_inputs()

    def _L0_cond_setup():
        import jax, jax.numpy as jnp
        import numpy as np
        NEG_INF = -1e+30
        key = jax.random.key(seed)
        k1, k2, k3, k4, k5 = jax.random.split(key, 5)
        B, S, D, A = (16, 256, 256, 64)
        hidden = jax.random.normal(k1, (B, S, D), dtype=jnp.float32)
        W1 = jax.random.normal(k2, (D, A), dtype=jnp.float32) / np.sqrt(D)
        b1 = jax.random.normal(k3, (A,), dtype=jnp.float32) * 0.01
        v = jax.random.normal(k4, (A,), dtype=jnp.float32) / np.sqrt(A)
        prompt_type_ids = jax.random.randint(k5, (B,), 0, 3, dtype=jnp.int32)
        return {'hidden': hidden, 'W1': W1, 'b1': b1, 'v': v, 'prompt_type_ids': prompt_type_ids}
    _L0_cond_all = _L0_cond_setup()
    _L0_cond_in = {k: v for k, v in _L0_cond_all.items() if k in ('W1', 'b1', 'v')}
    del _L0_cond_all

    def _L1_cond_setup():
        import jax, jax.numpy as jnp
        import numpy as np
        C, I, O = (32, 256, 256)
        B, T = (64, 128)
        key = jax.random.key(seed)
        kx, kc, kw, kb = jax.random.split(key, 4)
        x = jax.random.normal(kx, (B, T, I), dtype=jnp.float32)
        cat_ids = jax.random.randint(kc, (B,), 0, C)
        W = 0.02 * jax.random.normal(kw, (C, I, O), dtype=jnp.float32)
        b = jnp.zeros((C, O), dtype=jnp.float32)
        return {'x': x, 'cat_ids': cat_ids, 'W': W, 'b': b}
    _L1_cond_all = _L1_cond_setup()
    _L1_cond_in = {k: v for k, v in _L1_cond_all.items() if k in ('W', 'b')}
    del _L1_cond_all

    def _L2_cond_setup():
        import jax, jax.numpy as jnp
        import numpy as np
        B, S, D, F = (32, 128, 256, 1024)
        R_COMMON, R_DOMAIN, E = (16, 16, 8)
        ALPHA = 2.0

        def _expert_lora(x, expert_ids, Wa, Wb):
            Ab = Wa[expert_ids]
            Bb = Wb[expert_ids]
            low = jnp.einsum('bsd,brd->bsr', x, Ab)
            return ALPHA * jnp.einsum('bsr,bor->bso', low, Bb)
        key = jax.random.key(seed)
        ks = jax.random.split(key, 12)
        sd = lambda k, shape: jax.random.normal(k, shape, dtype=jnp.float32) * (1.0 / np.sqrt(shape[-1]))
        return {'hidden_states': jax.random.normal(ks[0], (B, S, D), dtype=jnp.float32), 'expert_ids': jax.random.randint(ks[1], (B,), 0, E, dtype=jnp.int32), 'wi': sd(ks[2], (F, D)), 'wo': sd(ks[3], (D, F)), 'common_wi_a': sd(ks[4], (R_COMMON, D)), 'common_wi_b': sd(ks[5], (F, R_COMMON)), 'common_wo_a': sd(ks[6], (R_COMMON, F)), 'common_wo_b': sd(ks[7], (D, R_COMMON)), 'experts_wi_a': sd(ks[8], (E, R_DOMAIN, D)), 'experts_wi_b': sd(ks[9], (F, R_DOMAIN)) * jnp.ones((E, 1, 1)) * 0.0 + sd(ks[9], (E, F, R_DOMAIN)), 'experts_wo_a': sd(ks[10], (E, R_DOMAIN, F)), 'experts_wo_b': sd(ks[11], (E, D, R_DOMAIN))}
    _L2_cond_all = _L2_cond_setup()
    _L2_cond_in = {k: v for k, v in _L2_cond_all.items() if k in ('wi', 'wo', 'common_wi_a', 'common_wi_b', 'common_wo_a', 'common_wo_b', 'experts_wi_a', 'experts_wi_b', 'experts_wo_a', 'experts_wo_b')}
    del _L2_cond_all

    def _L3_cond_setup():
        import jax, jax.numpy as jnp
        import numpy as np
        key = jax.random.key(seed)
        k1, k2, k3, k4 = jax.random.split(key, 4)
        B, H, W = (64, 256, 256)
        return {'y': jax.random.uniform(k1, (B, H, W), dtype=jnp.float32), 'zX': jax.random.uniform(k2, (B, 1), dtype=jnp.float32), 'zY': jax.random.uniform(k3, (B, 1), dtype=jnp.float32), 'zR': jax.random.uniform(k4, (B, 1), dtype=jnp.float32), 'dx': 1, 'dy': 1}
    _L3_cond_all = _L3_cond_setup()
    _L3_cond_in = {k: v for k, v in _L3_cond_all.items() if k in ()}
    del _L3_cond_all
    return {'x': x, 'itok_B_0_2': itok_B_0_2, 'itok_B_0_30': itok_B_0_30, 'itok_B_0_7': itok_B_0_7, 'condB_zX': condB_zX, 'condB_zY': condB_zY, 'condB_zR': condB_zR, 'L0_cond_W1': _L0_cond_in['W1'], 'L0_cond_b1': _L0_cond_in['b1'], 'L0_cond_v': _L0_cond_in['v'], 'L1_cond_W': _L1_cond_in['W'], 'L1_cond_b': _L1_cond_in['b'], 'L2_cond_wi': _L2_cond_in['wi'], 'L2_cond_wo': _L2_cond_in['wo'], 'L2_cond_common_wi_a': _L2_cond_in['common_wi_a'], 'L2_cond_common_wi_b': _L2_cond_in['common_wi_b'], 'L2_cond_common_wo_a': _L2_cond_in['common_wo_a'], 'L2_cond_common_wo_b': _L2_cond_in['common_wo_b'], 'L2_cond_experts_wi_a': _L2_cond_in['experts_wi_a'], 'L2_cond_experts_wi_b': _L2_cond_in['experts_wi_b'], 'L2_cond_experts_wo_a': _L2_cond_in['experts_wo_a'], 'L2_cond_experts_wo_b': _L2_cond_in['experts_wo_b']}

def reference(x, itok_B_0_2, itok_B_0_30, itok_B_0_7, condB_zX, condB_zY, condB_zR, L0_cond_W1, L0_cond_b1, L0_cond_v, L1_cond_W, L1_cond_b, L2_cond_wi, L2_cond_wo, L2_cond_common_wi_a, L2_cond_common_wi_b, L2_cond_common_wo_a, L2_cond_common_wo_b, L2_cond_experts_wi_a, L2_cond_experts_wi_b, L2_cond_experts_wo_a, L2_cond_experts_wo_b):
    import jax
    import jax.numpy as jnp

    def _L0_cond_ref(hidden, W1, b1, v, prompt_type_ids):
        import jax, jax.numpy as jnp
        import numpy as np
        NEG_INF = -1e+30
        B, S, D = hidden.shape
        attn_in = jnp.tanh(jnp.einsum('bsd,da->bsa', hidden, W1) + b1)
        scores = jnp.einsum('bsa,a->bs', attn_in, v)
        idx = jnp.arange(S)
        j = idx[:, None]
        l = idx[None, :]
        prefix_m = l <= j
        postfix_m = l >= j
        cloze_m = l != j
        pt = prompt_type_ids[:, None, None]
        mask = jnp.where(pt == 0, prefix_m[None], jnp.where(pt == 1, postfix_m[None], cloze_m[None]))
        masked_scores = jnp.where(mask, scores[:, None, :], NEG_INF)
        p = jax.nn.softmax(masked_scores, axis=-1)
        cnt = jnp.sum(mask, axis=-1).astype(hidden.dtype)
        pooled = jnp.einsum('bjl,bld->bjd', p, hidden) / cnt[..., None]
        return pooled

    def _L1_cond_ref(x, cat_ids, W, b):
        import jax, jax.numpy as jnp
        import numpy as np
        C, I, O = (32, 256, 256)
        B, T = (64, 128)
        selected_W = W[cat_ids]
        selected_b = b[cat_ids]
        if x.ndim == 2:
            return jnp.einsum('bi,bio->bo', x, selected_W) + selected_b
        return jnp.einsum('bti,bio->bto', x, selected_W) + selected_b[:, None, :]

    def _L2_cond_ref(hidden_states, expert_ids, wi, wo, common_wi_a, common_wi_b, common_wo_a, common_wo_b, experts_wi_a, experts_wi_b, experts_wo_a, experts_wo_b):
        import jax, jax.numpy as jnp
        import numpy as np
        B, S, D, F = (32, 128, 256, 1024)
        R_COMMON, R_DOMAIN, E = (16, 16, 8)
        ALPHA = 2.0

        def _expert_lora(x, expert_ids, Wa, Wb):
            Ab = Wa[expert_ids]
            Bb = Wb[expert_ids]
            low = jnp.einsum('bsd,brd->bsr', x, Ab)
            return ALPHA * jnp.einsum('bsr,bor->bso', low, Bb)
        x = hidden_states
        hidden_i = jnp.einsum('bsd,fd->bsf', x, wi)
        hidden_i += ALPHA * jnp.einsum('bsr,fr->bsf', jnp.einsum('bsd,rd->bsr', x, common_wi_a), common_wi_b)
        hidden_i += _expert_lora(x, expert_ids, experts_wi_a, experts_wi_b)
        hidden_i = jax.nn.relu(hidden_i)
        hidden_o = jnp.einsum('bsf,df->bsd', hidden_i, wo)
        hidden_o += ALPHA * jnp.einsum('bsr,dr->bsd', jnp.einsum('bsf,rf->bsr', hidden_i, common_wo_a), common_wo_b)
        hidden_o += _expert_lora(hidden_i, expert_ids, experts_wo_a, experts_wo_b)
        return hidden_o

    def _L3_cond_ref(y, zX, zY, zR, dx, dy):
        import jax, jax.numpy as jnp
        import numpy as np
        yp_x = jnp.pad(y, ((0, 0), (0, 0), (1, 1)), mode='reflect')
        lap_x = (yp_x[:, :, :-2] - 2.0 * y + yp_x[:, :, 2:]) / (dx * dx)
        yp_y = jnp.pad(y, ((0, 0), (1, 1), (0, 0)), mode='reflect')
        lap_y = (yp_y[:, :-2, :] - 2.0 * y + yp_y[:, 2:, :]) / (dy * dy)
        du_dt = zX[:, :, None] * lap_x + zY[:, :, None] * lap_y + zR[:, :, None] * y * (1.0 - y)
        return du_dt
    x = x + _L0_cond_ref(x, L0_cond_W1, L0_cond_b1, L0_cond_v, itok_B_0_2)
    x = x + _L1_cond_ref(x, itok_B_0_30, L1_cond_W, L1_cond_b)
    x = x + _L2_cond_ref(x, itok_B_0_7, L2_cond_wi, L2_cond_wo, L2_cond_common_wi_a, L2_cond_common_wi_b, L2_cond_common_wo_a, L2_cond_common_wo_b, L2_cond_experts_wi_a, L2_cond_experts_wi_b, L2_cond_experts_wo_a, L2_cond_experts_wo_b)
    x = x + _L3_cond_ref(x, condB_zX[:, None], condB_zY[:, None], condB_zR[:, None], 1, 1)
    return x

_drawn_inputs = setup_inputs


def setup_inputs(seed=0):
    import zlib

    import numpy as np

    out = dict(_drawn_inputs(seed))
    spreads = {'L1_cond_b': (0.0, 0.1)}
    factors = {'L0_cond_W1': 5.274, 'L0_cond_b1': 200.0, 'L0_cond_v': 8.0}
    for name, (base, spread) in spreads.items():
        noise = np.random.default_rng([zlib.crc32(name.encode()), seed]).standard_normal(out[name].shape)
        drawn = base * np.exp(spread * noise) if base else spread * noise
        out[name] = jnp.asarray(drawn.astype(out[name].dtype))
    for name, factor in factors.items():
        out[name] = (out[name] * factor).astype(out[name].dtype)
    return out
```

```python
from contextlib import ExitStack

import concourse.bass as bass
from concourse import mybir

F32 = mybir.dt.float32
F32R = mybir.dt.float32r
BF16 = mybir.dt.bfloat16
I32 = mybir.dt.int32
ALU = mybir.AluOpType
ACT = mybir.ActivationFunctionType
ds = bass.ds

P = 128
B, S, D = 8, 512, 256
A = 64
F = 1024
C = D // P
J = S // P
KF = F // P
LORA_ALPHA = 2.0
R = 32
ND = D + 2
NCAT, NEXP = 31, 8
XR = 4
Q = 32
NEG = -1e30

CF_ID, CF_SHIFT, CF_RES, CF_TOK = 0, P, 3 * P, 3 * P + C * D
CF_LO, CF_SIGN = CF_TOK + J, CF_TOK + J + 2
CF_N = CF_SIGN + 2
CB_ID, CB_LO, CB_UP, CB_BLO, CB_BUP, CB_HOT = 0, P, 2 * P, 3 * P, 3 * P + S, 3 * P + 2 * S
CB_N = CB_HOT + B * J
ALPHA_N = D + F
BETA_N = F + D


def need(eng, sem, value):
    if isinstance(value, int) and value <= 0:
        return
    eng.wait_ge(sem, value)


def build(nc, xT_d, xn_d, cf_d, cb_d, typeq_d, types_d, ids_d, z_d, w1_d, b1v_d, wc_d, bc_d, wi_d, wo_d,
          la_common_d, la_expert_d, lb_common_d, lb_expert_d, out_d):
    with ExitStack() as ctx:
        def sb(name, shape, dt=F32):
            return ctx.enter_context(nc.sbuf_tensor(name, shape, dt))

        def bank(name):
            return ctx.enter_context(nc.psum_tensor(name, [P, S], F32))

        def sem(name):
            return ctx.enter_context(nc.semaphore(name))

        cf = sb("cf", [P, CF_N])
        cb = sb("cb", [P, CB_N], BF16)
        typeq_i = sb("typeq_i", [P, 1], I32)
        types_i = sb("types_i", [P, B], I32)
        ids = sb("ids", [1, 2 * B], I32)
        typeq = sb("typeq", [P, 1])
        types = sb("types", [P, B])
        rowc = sb("rowc", [P, 4])
        rowneg = sb("rowneg", [P, 2])
        batc = sb("batc", [P, 4, B])
        batneg = sb("batneg", [P, 3, B])
        cnt_a = sb("cnt_a", [P, B])
        cnt_b = sb("cnt_b", [P, B])
        cnt = sb("cnt", [P, B, J])
        z = sb("z", [P, 3, B])
        zc = sb("zc", [P, 3, B])
        w1 = sb("w1", [P, C, A])
        b1v = sb("b1v", [A, 2])
        sel = sb("sel", [P, B * J, P], BF16)
        diagmask = sb("diagmask", [P, B, P], BF16)
        m3 = sb("m3", [P, S], BF16)
        scol = sb("scol", [P, J, 3 * Q])
        scratch = sb("scratch", [P, 4 * C * S])
        tanhT = sb("tanhT", [A, 2, S])
        xn = sb("xn", [P, 2, J, D])
        h_hi = sb("h_hi", [P, J, ND], F32R)
        h_lo = sb("h_lo", [P, J, ND], F32R)
        p_raw = sb("p_raw", [P, 2, S])
        p_hi = sb("p_hi", [P, J, S], F32R)
        p_lo = sb("p_lo", [P, J, S], F32R)
        den = sb("den", [P, 2, J])
        x1n = sb("x1n", [P, J, D])
        x1_hi = sb("x1_hi", [P, C, S], F32R)
        x1_lo = sb("x1_lo", [P, C, S], F32R)
        wc_raw = sb("wc_raw", [P, C, D])
        wc_res = sb("wc_res", [P, C, D])
        wc_hi = sb("wc_hi", [P, C, D], F32R)
        wc_lo = sb("wc_lo", [P, C, D], F32R)
        bc = sb("bc", [P, 2, C])
        x2 = sb("x2", [P, 2, C, S])
        x2_hi = sb("x2_hi", [P, C, S], F32R)
        x2_lo = sb("x2_lo", [P, C, S], F32R)
        wi = sb("wi", [P, C, F])
        wo = sb("wo", [P, KF, D])
        w_sum = sb("w_sum", [P, 2, S])
        wi_hi = sb("wi_hi", [P, C, F], F32R)
        wi_lo = sb("wi_lo", [P, C, F], F32R)
        wo_hi = sb("wo_hi", [P, KF, D], F32R)
        wo_lo = sb("wo_lo", [P, KF, D], F32R)
        la_raw = sb("la_raw", [P, ALPHA_N])
        lb_raw = sb("lb_raw", [P, BETA_N])
        la = sb("la", [P, ALPHA_N], F32R)
        lb = sb("lb", [P, BETA_N], F32R)
        hid_hi = sb("hid_hi", [P, 2, S], F32R)
        hid_lo = sb("hid_lo", [P, 2, S], F32R)
        x3 = sb("x3", [P, C, S])

        xT = scratch[:, :].rearrange("p (r c s) -> p r c s", r=XR, c=C)
        t_lin, t_quad, t_y, t_out = (xT[:, i] for i in range(4))
        srow = p_raw[0:3 * Q, 0, :]
        premax = p_raw[0:3 * Q, 1, :]
        postmax = x1n[0:3 * Q, 0:2, :].rearrange("p a b -> p (a b)")
        exmax = x1n[0:3 * Q, 2:4, :].rearrange("p a b -> p (a b)")
        negmax = w_sum[0:3 * Q, 0, :]
        rest = w_sum[0:3 * Q, 1, :]
        mid = sb("mid", [3 * Q, S], BF16)

        xb = [bank("xb0"), bank("xb1")]
        tb_ = ctx.enter_context(nc.psum_tensor("tb", [P, C, S], F32))
        ob = ctx.enter_context(nc.psum_tensor("ob", [P, C, S], F32))
        rb = [bank("rb0"), bank("rb1")]

        names = """ld_cf ld_cb ld_small ld_w1 ld_wi ld_wo ld_common ld_xn ld_wc ld_lora ld_ids
        proj_mm score_mm turned tanh_done scol_done consts_done pool_consts m3_done srow_used
        logit_mm num_mm turn_mm l1_mm fold_mm hid_mm out_mm lap_mm
        h_hi_done exp_done x1_hi_done x2_done x2_hi_done hid_hi_done w_hi_done lin_done wc_hi_done
        h_lo_done p_hi_done p_lo_done x1_done x1_lo_done x2_lo_done hid_lo_done w_sum_done x3_done quad_done
        out_done dve_step
        scol_zero ones_done den_step quad_step
        lora_hi_done lora_done wc_res_done wc_lo_done w_lo_done y_done pool_step
        stored""".split()
        s = {n: sem(n) for n in names}
        ld_xT = [sem(f"ld_xT{i}") for i in range(XR)]

        block = ctx.enter_context(nc.Block())

        FOLDS = [("wi", 0, 0), ("wi", 1, 0), ("wo", 0), ("wi", 0, 1), ("wo", 1), ("wo", 2), ("wi", 1, 1), ("wo", 3)]
        NFOLD = len(FOLDS)
        fold_at = {f: i for i, f in enumerate(FOLDS)}

        def wfold(f, part):
            if f[0] == "wi":
                return {"raw": wi, "hi": wi_hi, "lo": wi_lo}[part][:, f[1], f[2] * S:(f[2] + 1) * S]
            return {"raw": wo, "hi": wo_hi, "lo": wo_lo}[part][:, 2 * f[1]:2 * f[1] + 2, :].rearrange("p k d -> p (k d)")

        @block.sync
        def _(sp):
            def load_xT(b):
                if b >= XR:
                    sp.wait_ge(s["proj_mm"], b - XR + 1)
                sp.dma_start(xT[:, b % XR], xT_d[b]).then_inc(ld_xT[b % XR], 16)

            def load_xn(n, slot):
                need(sp, s["h_lo_done"], n)
                sp.dma_start(xn[:, ds(slot, 1)], xn_d[ds(n, 1)].rearrange("b p j d -> p b j d")).then_inc(s["ld_xn"], 16)

            def load_wc(n, slot):
                cat = sp.value_load(ids[0:1, ds(n, 1)], min_val=0, max_val=NCAT)
                need(sp, s["wc_res_done"], n)
                need(sp, s["x2_done"], n - 1)
                sp.dma_start(wc_raw[:, :, :], wc_d[ds(cat, 1)].rearrange("e p c d -> (e p) c d")).then_inc(s["ld_wc"], 16)
                sp.dma_start(bc[:, ds(slot, 1)], bc_d[ds(cat, 1)].rearrange("e p c -> p e c")).then_inc(s["ld_wc"], 16)

            def load_lora(n):
                expert = sp.value_load(ids[0:1, ds(n + B, 1)], min_val=0, max_val=NEXP - 1)
                need(sp, s["lora_done"], 2 * n)
                for raw, expert_d in ((la_raw, la_expert_d), (lb_raw, lb_expert_d)):
                    for q in range(4):
                        sp.dma_start(raw[Q * q + R // 2:Q * q + R, :],
                                     expert_d[ds(expert, 1)].rearrange("e r n -> (e r) n")).then_inc(s["ld_lora"], 16)

            sp.dma_start(w1[:, :, :], w1_d).then_inc(s["ld_w1"], 16)
            sp.dma_start(b1v[:, :], b1v_d).then_inc(s["ld_w1"], 16)
            load_xT(0)
            load_xT(1)
            sp.dma_start(typeq_i[:, :], typeq_d).then_inc(s["ld_small"], 16)
            sp.dma_start(types_i[:, :], types_d).then_inc(s["ld_small"], 16)
            sp.dma_start(z[:, :, :], z_d).then_inc(s["ld_small"], 16)
            sp.dma_start(cb[:, :], cb_d).then_inc(s["ld_cb"], 16)
            sp.dma_start(ids[:, :], ids_d).then_inc(s["ld_ids"], 16)
            load_xT(2)
            sp.dma_start(cf[:, :], cf_d).then_inc(s["ld_cf"], 16)
            load_xT(3)
            for raw, common_d in ((la_raw, la_common_d), (lb_raw, lb_common_d)):
                for q in range(4):
                    sp.dma_start(raw[Q * q:Q * q + R // 2, :], common_d).then_inc(s["ld_common"], 16)
            sp.wait_ge(s["ld_ids"], 16)
            load_lora(0)
            load_xT(4)
            sp.dma_start(wi[:, :, :], wi_d).then_inc(s["ld_wi"], 16)
            load_xT(5)
            sp.dma_start(wo[:, :, :], wo_d).then_inc(s["ld_wo"], 16)
            load_xT(6)
            load_xT(7)
            load_xn(0, 0)
            load_wc(0, 0)
            load_xn(1, 1)

            def store(n):
                sp.wait_ge(s["out_done"], n + 1)
                sp.dma_start(out_d[ds(n, 1)].rearrange("b p c s -> (b p) c s"), t_out).then_inc(s["stored"], 16)

            def step(b, stores=True, xn_left=True):
                slot = b & 1
                load_wc(b + 1, 1 - slot)
                load_lora(b + 1)
                if stores:
                    store(b - 1)
                if xn_left:
                    load_xn(b + 2, slot)

            step(0, stores=False)
            with sp.Fori(1, B - 2) as b:
                step(b)
            step(B - 2, xn_left=False)
            store(B - 2)
            store(B - 1)
            sp.wait_ge(s["stored"], 16 * B)

        @block.tensor
        def _(pe):
            def split_matmul(out, w_hi, w_lo, x_hi, x_lo, first, last):
                pe.matmul(out, w_hi, x_hi, start=first, stop=False)
                pe.matmul(out, w_hi, x_lo, start=False, stop=False)
                return pe.matmul(out, w_lo, x_hi, start=False, stop=last)

            def project(b):
                pe.wait_ge(ld_xT[b % XR], 16 * (b // XR + 1))
                if b >= 2:
                    pe.wait_ge(s["tanh_done"], b - 1)
                for c in range(C):
                    mm = pe.matmul(rb[b % 2][0:A, :], w1[:, c, :], xT[:, b % XR, c, :], start=c == 0, stop=c == C - 1)
                mm.then_inc(s["proj_mm"], 1)

            def score(b):
                pe.wait_ge(s["tanh_done"], b + 1)
                if b >= 2:
                    pe.wait_ge(s["scol_done"], b - 1)
                for j in range(J):
                    mm = pe.matmul(xb[b % 2][:, j:j + 1], tanhT[:, b % 2, j * P:(j + 1) * P], b1v[:, 1:2],
                                   start=True, stop=True)
                mm.then_inc(s["score_mm"], 1)

            def score_rows():
                pe.wait_ge(s["scol_done"], B)
                for j in range(J):
                    mm = pe.transpose(tb_[0:3 * Q, 0, j * P:(j + 1) * P], scol[:, j, :], cf[:, CF_ID:CF_ID + P])
                mm.then_inc(s["turned"], 1)

            def logits(n, l):
                if l < 2:
                    need(pe, s["x2_done"], n)
                    if isinstance(n, int) and n == 0 and l == 0:
                        pe.wait_ge(s["m3_done"], 1)
                        pe.wait_ge(s["pool_consts"], 1)
                else:
                    pe.wait_ge(s["exp_done"], n * J + l - 1)
                out = xb[l % 2]
                pe.matmul(out[:, :], sel[:, ds(n * J + l, 1), :].rearrange("p o m -> p (o m)"), m3[:, :], start=True, stop=False,
                          skip_group_check=True)
                pe.matmul(out[:, l * P:(l + 1) * P], cb[:, CB_ID:CB_ID + P],
                          diagmask[:, ds(n, 1), :].rearrange("p o m -> p (o m)"), start=False, stop=True,
                          skip_group_check=True).then_inc(s["logit_mm"], 1)

            def pool_block(n, j):
                if j == 0:
                    pe.wait_ge(s["p_hi_done"], J * n + J)
                    pe.wait_ge(s["p_lo_done"], J * n + J)
                    pe.wait_ge(s["h_hi_done"], n + 1)
                    pe.wait_ge(s["h_lo_done"], n + 1)
                    if isinstance(n, int) and n == 0:
                        pe.wait_ge(s["ones_done"], 2)
                if j < 2:
                    pe.wait_ge(s["exp_done"], J * n + J)
                else:
                    pe.wait_ge(s["x1_done"], J * n + j - 1)
                for l in range(J):
                    mm = split_matmul(xb[j % 2][:, 0:ND], p_hi[:, l, j * P:(j + 1) * P], p_lo[:, l, j * P:(j + 1) * P],
                                      h_hi[:, l, :], h_lo[:, l, :], l == 0, l == J - 1)
                mm.then_inc(s["num_mm"], 1)

            def turn(n, j):
                pe.wait_ge(s["x1_done"], J * n + j + 1)
                if j == 0:
                    need(pe, s["quad_done"], n - 1)
                    need(pe, s["w_sum_done"], NFOLD * n)
                for c in range(C):
                    mm = pe.transpose(tb_[:, c, j * P:(j + 1) * P], x1n[:, j, c * P:(c + 1) * P], cf[:, CF_ID:CF_ID + P])
                mm.then_inc(s["turn_mm"], 1)

            def layer1(n):
                pe.wait_ge(s["x1_hi_done"], n + 1)
                pe.wait_ge(s["x1_lo_done"], n + 1)
                pe.wait_ge(s["wc_hi_done"], n + 1)
                pe.wait_ge(s["wc_lo_done"], n + 1)
                for co in range(C):
                    for c in range(C):
                        cols = slice(co * P, (co + 1) * P)
                        mm = split_matmul(xb[co][:, :], wc_hi[:, c, cols], wc_lo[:, c, cols], x1_hi[:, c, :], x1_lo[:, c, :],
                                          c == 0, c == C - 1)
                    mm.then_inc(s["l1_mm"], 1)

            def fold(n, f):
                i = fold_at[f]
                if i == 0:
                    pe.wait_ge(s["lora_done"], 2 * (n + 1))
                if i < 2:
                    if isinstance(n, int) and n == 0:
                        pe.wait_ge(s["srow_used"], 1)
                    else:
                        pe.wait_ge(s["x1_lo_done"], n + 1)
                else:
                    pe.wait_ge(s["w_sum_done"], NFOLD * n + i - 1)
                if f[0] == "wi":
                    mm = pe.matmul(tb_[:, i % 2, :], la[:, f[1] * P:(f[1] + 1) * P], lb[:, f[2] * S:(f[2] + 1) * S],
                                   start=True, stop=True)
                else:
                    for k in range(2):
                        kf = 2 * f[1] + k
                        mm = pe.matmul(tb_[:, i % 2, k * D:(k + 1) * D], la[:, D + kf * P:D + (kf + 1) * P], lb[:, F:F + D],
                                       start=True, stop=True)
                mm.then_inc(s["fold_mm"], 1)

            def hidden(b, k):
                if k == 0:
                    pe.wait_ge(s["x2_hi_done"], b + 1)
                    pe.wait_ge(s["x2_lo_done"], b + 1)
                if k % (KF // 2) == 0:
                    ready = NFOLD * b + fold_at[("wi", 1, k // (KF // 2))] + 1
                    pe.wait_ge(s["w_hi_done"], ready)
                    pe.wait_ge(s["w_lo_done"], ready)
                need(pe, s["hid_lo_done"], KF * b + k - 1)
                for c in range(C):
                    cols = slice(k * P, (k + 1) * P)
                    mm = split_matmul(rb[k % 2][:, :], wi_hi[:, c, cols], wi_lo[:, c, cols], x2_hi[:, c, :], x2_lo[:, c, :],
                                      c == 0, c == C - 1)
                mm.then_inc(s["hid_mm"], 1)

            def output(b, k):
                if k == 0:
                    need(pe, s["x3_done"], b)
                if k % 2 == 0:
                    ready = NFOLD * b + fold_at[("wo", k // 2)] + 1
                    pe.wait_ge(s["w_hi_done"], ready)
                    pe.wait_ge(s["w_lo_done"], ready)
                pe.wait_ge(s["hid_hi_done"], KF * b + k + 1)
                pe.wait_ge(s["hid_lo_done"], KF * b + k + 1)
                for c in range(C):
                    cols = slice(c * P, (c + 1) * P)
                    mm = split_matmul(ob[:, c, :], wo_hi[:, k, cols], wo_lo[:, k, cols], hid_hi[:, k % 2, :],
                                      hid_lo[:, k % 2, :], k == 0, k == KF - 1)
                mm.then_inc(s["out_mm"], 1)

            def neighbours(b):
                pe.wait_ge(s["x3_done"], b + 1)
                if isinstance(b, int) and b == B - 1:
                    pe.wait_ge(s["quad_done"], B - 1)
                else:
                    pe.wait_ge(s["w_sum_done"], NFOLD * (b + 2))
                for c in range(C):
                    shift = cf[:, CF_SHIFT + c * P:CF_SHIFT + (c + 1) * P]
                    mm = pe.matmul(tb_[:, c, :], shift, x3[:, 1 - c, :], start=True, stop=True)
                mm.then_inc(s["lap_mm"], 1)

            pe.wait_ge(s["ld_w1"], 32)
            for b in range(B):
                project(b)
                if b >= 1:
                    score(b - 1)
            score(B - 1)
            pe.wait_ge(s["ld_cf"], 16)
            score_rows()
            for f in FOLDS:
                fold(0, f)
            for l in range(J):
                logits(0, l)
            for j in range(J):
                pool_block(0, j)
                if j >= 1:
                    turn(0, j - 1)
            turn(0, J - 1)
            layer1(0)

            def step(b):
                n = b + 1
                hidden(b, 0)
                if not (isinstance(b, int) and b == 0):
                    neighbours(b - 1)
                hidden(b, 1)
                logits(n, 0)
                output(b, 0)
                hidden(b, 2)
                logits(n, 1)
                output(b, 1)
                hidden(b, 3)
                logits(n, 2)
                output(b, 2)
                hidden(b, 4)
                logits(n, 3)
                output(b, 3)
                pool_block(n, 0)
                pool_block(n, 1)
                turn(n, 0)
                pool_block(n, 2)
                turn(n, 1)
                hidden(b, 5)
                output(b, 4)
                pool_block(n, 3)
                turn(n, 2)
                turn(n, 3)
                hidden(b, 6)
                output(b, 5)
                layer1(n)
                fold(n, FOLDS[0])
                fold(n, FOLDS[1])
                hidden(b, 7)
                fold(n, FOLDS[2])
                fold(n, FOLDS[3])
                output(b, 6)
                fold(n, FOLDS[4])
                fold(n, FOLDS[5])
                fold(n, FOLDS[6])
                output(b, 7)
                fold(n, FOLDS[7])

            step(0)
            with pe.Fori(1, B - 1) as b:
                step(b)
            hidden(B - 1, 0)
            neighbours(B - 2)
            for k in range(1, KF):
                hidden(B - 1, k)
                output(B - 1, k - 1)
            output(B - 1, KF - 1)
            neighbours(B - 1)

        @block.scalar
        def _(act):
            def split_h(n):
                act.wait_ge(s["ld_xn"], 16 * (n + 1))
                need(act, s["num_mm"], J * n)
                act.activation(h_hi[:, :, 0:D], xn[:, ds(n & 1, 1)].rearrange("p o j d -> p (o j) d"),
                               ACT.Copy).then_inc(s["h_hi_done"], 1)

            def exps(n, l):
                act.wait_ge(s["logit_mm"], J * n + l + 1)
                need(act, s["p_lo_done"], J * n + l - 1)
                act.activation(p_raw[:, l % 2, :], xb[l % 2][:, :], ACT.Exp,
                               bias=scol[:, l, ds(n, 1)]).then_inc(s["exp_done"], 1)

            def split_x1(n):
                act.wait_ge(s["turn_mm"], J * (n + 1))
                need(act, s["l1_mm"], C * n)
                act.activation(x1_hi[:, :, :], tb_[:, :, :], ACT.Copy).then_inc(s["x1_hi_done"], 1)

            def bias_x2(n):
                need(act, s["x3_done"], n - 1)
                for c in range(C):
                    act.wait_ge(s["l1_mm"], C * n + c + 1)
                    ins = act.activation(x2[:, ds(n & 1, 1), c, :].rearrange("p o s -> p (o s)"), xb[c][:, :], ACT.Identity,
                                         bias=bc[:, ds(n & 1, 1), c])
                ins.then_inc(s["x2_done"], 1)

            def split_wc(n):
                act.wait_ge(s["wc_res_done"], n + 1)
                need(act, s["l1_mm"], C * n)
                act.activation(wc_hi[:, :, :], wc_res[:, :, :], ACT.Copy).then_inc(s["wc_hi_done"], 1)

            def round_lora(n):
                act.wait_ge(s["ld_lora"], 8 * 16 * (n + 1))
                need(act, s["fold_mm"], NFOLD * n)
                act.activation(la[:, :], la_raw[:, :], ACT.Copy, scale=cf[:, CF_SIGN:CF_SIGN + 1]).then_inc(s["lora_hi_done"], 1)
                act.activation(lb[:, :], lb_raw[:, :], ACT.Copy, scale=cf[:, CF_SIGN + 1:CF_SIGN + 2]).then_inc(s["lora_hi_done"], 1)

            def relu_hidden(b, k):
                act.wait_ge(s["hid_mm"], KF * b + k + 1)
                need(act, s["out_mm"], KF * b + k - 1)
                act.activation(hid_hi[:, k % 2, :], rb[k % 2][:, :], ACT.Relu).then_inc(s["hid_hi_done"], 1)

            def split_w(n, i):
                act.wait_ge(s["w_sum_done"], NFOLD * n + i + 1)
                act.activation(wfold(FOLDS[i], "hi"), w_sum[:, i % 2, :], ACT.Copy).then_inc(s["w_hi_done"], 1)

            def linear(b):
                act.wait_ge(s["x3_done"], b + 1)
                need(act, s["quad_done"], b)
                act.activation(t_lin, x3[:, :, :], ACT.Identity, bias=zc[:, 1, ds(b, 1)],
                               scale=zc[:, 2, ds(b, 1)]).then_inc(s["lin_done"], 1)

            act.wait_ge(s["ld_w1"], 32)
            for b in range(B):
                act.wait_ge(s["proj_mm"], b + 1)
                if b >= 2:
                    act.wait_ge(s["score_mm"], b - 1)
                act.activation(tanhT[:, b % 2, :], rb[b % 2][0:A, :], ACT.Tanh, bias=b1v[:, 0:1]).then_inc(s["tanh_done"], 1)
            act.wait_ge(s["ld_cf"], 16)
            act.wait_ge(s["ld_common"], 8 * 16)
            round_lora(0)
            split_h(0)
            for i in range(NFOLD):
                split_w(0, i)
            split_wc(0)
            for l in range(J):
                exps(0, l)
            split_x1(0)
            bias_x2(0)

            def step(b, last=False):
                n = b + 1
                relu_hidden(b, 0)
                if isinstance(b, int) and b == 0:
                    act.wait_ge(s["consts_done"], 1)
                else:
                    linear(b - 1)
                if last:
                    for k in range(1, KF):
                        relu_hidden(b, k)
                    return
                relu_hidden(b, 1)
                exps(n, 0)
                round_lora(n)
                relu_hidden(b, 2)
                exps(n, 1)
                relu_hidden(b, 3)
                exps(n, 2)
                relu_hidden(b, 4)
                exps(n, 3)
                split_h(n)
                split_wc(n)
                relu_hidden(b, 5)
                relu_hidden(b, 6)
                split_x1(n)
                bias_x2(n)
                split_w(n, 0)
                split_w(n, 1)
                relu_hidden(b, 7)
                for i in range(2, NFOLD):
                    split_w(n, i)

            step(0)
            with act.Fori(1, B - 1) as b:
                step(b)
            step(B - 1, last=True)
            linear(B - 1)

        @block.vector
        def _(v):
            steps = [0]

            def link(ins):
                ins.then_inc(s["dve_step"], 1)
                steps[0] += 1
                v.wait_ge(s["dve_step"], steps[0])

            def scores_in(b):
                v.wait_ge(s["score_mm"], b + 1)
                src = xb[b % 2][:, 0:J].rearrange("p (j o) -> p j o", o=1).broadcast_to([P, J, 3])
                v.tensor_copy(scol[:, :, b:b + 2 * Q + 1:Q], src).then_inc(s["scol_done"], 1)

            def masks():
                v.wait_ge(s["ld_small"], 48)
                v.wait_ge(s["ld_cb"], 16)
                v.wait_ge(s["ld_cf"], 16)
                link(v.tensor_copy(types[:, :], types_i[:, :]))
                for col in range(2):
                    link(v.tensor_scalar(batc[:, col], types[:, :], float(col), None, ALU.is_equal))
                link(v.tensor_tensor(batc[:, 3], batc[:, 0], batc[:, 1], ALU.add))
                link(v.tensor_scalar(batc[:, 2], batc[:, 3], -1.0, 1.0, ALU.mult, ALU.add))
                link(v.tensor_scalar(batneg[:, :, :], batc[:, 0:3], NEG, None, ALU.mult))
                link(v.tensor_tensor(cnt_a[:, :], batc[:, 0], batc[:, 1], ALU.subtract))
                link(v.tensor_scalar(cnt_b[:, :], batc[:, 1], float(S + 1), None, ALU.mult))
                link(v.scalar_tensor_tensor(out=cnt_b[:, :], in0=batc[:, 2], scalar=float(S - 1), in1=cnt_b[:, :],
                                            op0=ALU.mult, op1=ALU.add))
                for j in range(J):
                    link(v.scalar_tensor_tensor(out=cnt[:, :, j], in0=cnt_a[:, :], scalar=cf[:, CF_TOK + j:CF_TOK + j + 1],
                                                in1=cnt_b[:, :], op0=ALU.mult, op1=ALU.add))
                link(v.tensor_tensor(zc[:, 0], z[:, 0], z[:, 1], ALU.add))
                link(v.tensor_scalar(zc[:, 1], zc[:, 0], -2.0, 1.0, ALU.mult, ALU.add))
                link(v.tensor_tensor(zc[:, 1], zc[:, 1], z[:, 2], ALU.add))
                link(v.tensor_scalar(zc[:, 2], z[:, 2], -1.0, None, ALU.mult))
                for b in range(B):
                    out = diagmask[:, b, :]
                    link(v.tensor_scalar(out, cb[:, CB_LO:CB_LO + P], batneg[:, 0, b:b + 1], None, ALU.mult))
                    link(v.scalar_tensor_tensor(out=out, in0=cb[:, CB_UP:CB_UP + P], scalar=batneg[:, 1, b:b + 1], in1=out,
                                                op0=ALU.mult, op1=ALU.add))
                    link(v.scalar_tensor_tensor(out=out, in0=cb[:, CB_ID:CB_ID + P], scalar=batneg[:, 2, b:b + 1], in1=out,
                                                op0=ALU.mult, op1=ALU.add))
                link(v.tensor_copy(typeq[:, :], typeq_i[:, :]))
                for col in range(2):
                    link(v.tensor_scalar(rowc[:, col:col + 1], typeq[:, :], float(col), None, ALU.is_equal))
                link(v.tensor_tensor(rowc[:, 3:4], rowc[:, 0:1], rowc[:, 1:2], ALU.add))
                link(v.tensor_scalar(rowc[:, 2:3], rowc[:, 3:4], -1.0, 1.0, ALU.mult, ALU.add))
                link(v.tensor_scalar(rowneg[:, :], rowc[:, 0:2], NEG, None, ALU.mult))
                link(v.tensor_scalar(rowc[:, 0:3], rowc[:, 0:3], -1.0, None, ALU.mult))
                q3 = slice(3 * Q, 4 * Q)
                link(v.tensor_scalar(m3[q3, :], cb[q3, CB_BLO:CB_BLO + S], rowneg[q3, 0:1], None, ALU.mult))
                link(v.scalar_tensor_tensor(out=m3[q3, :], in0=cb[q3, CB_BUP:CB_BUP + S], scalar=rowneg[q3, 1:2],
                                            in1=m3[q3, :], op0=ALU.mult, op1=ALU.add))
                v.memset(den[:, :, :], 0.0).then_inc(s["consts_done"], 1)

            def row_maxima():
                rows = slice(0, 3 * Q)
                v.wait_ge(s["turned"], 1)
                v.tensor_copy(srow, tb_[rows, 0, :]).then_inc(s["srow_used"], 1)
                v.wait_ge(s["srow_used"], 1)
                link(v.tensor_tensor_scan(premax, srow, srow, -3e38, ALU.max, ALU.max))
                link(v.tensor_tensor_scan(postmax[:, ::-1], srow[:, ::-1], srow[:, ::-1], -3e38, ALU.max, ALU.max))
                link(v.tensor_tensor(exmax[:, 1:S - 1], premax[:, 0:S - 2], postmax[:, 2:S], ALU.max))
                link(v.tensor_copy(exmax[:, 0:1], postmax[:, 1:2]))
                link(v.tensor_copy(exmax[:, S - 1:S], premax[:, S - 2:S - 1]))
                link(v.tensor_scalar(negmax, premax, rowc[rows, 0:1], None, ALU.mult))
                link(v.scalar_tensor_tensor(out=negmax, in0=postmax, scalar=rowc[rows, 1:2], in1=negmax, op0=ALU.mult, op1=ALU.add))
                link(v.scalar_tensor_tensor(out=negmax, in0=exmax, scalar=rowc[rows, 2:3], in1=negmax, op0=ALU.mult, op1=ALU.add))
                link(v.tensor_copy(m3[rows, :], negmax))
                link(v.tensor_tensor(rest, negmax, m3[rows, :], ALU.subtract))
                link(v.tensor_copy(mid[:, :], rest))
                link(v.tensor_tensor(rest, rest, mid[:, :], ALU.subtract))
                link(v.tensor_copy(m3[Q:2 * Q, :], mid[Q:2 * Q, :]))
                v.tensor_copy(m3[2 * Q:3 * Q, :], rest[2 * Q:3 * Q, :]).then_inc(s["m3_done"], 1)
                v.wait_ge(s["m3_done"], 1)

            def split_h(n):
                v.wait_ge(s["h_hi_done"], n + 1)
                need(v, s["num_mm"], J * n)
                v.tensor_tensor(h_lo[:, :, 0:D], xn[:, ds(n & 1, 1)].rearrange("p o j d -> p (o j) d"), h_hi[:, :, 0:D].bitcast(F32),
                                ALU.subtract).then_inc(s["h_lo_done"], 1)

            def split_p(n, l):
                v.wait_ge(s["exp_done"], J * n + l + 1)
                need(v, s["num_mm"], J * n)
                v.tensor_copy(p_hi[:, l, :], p_raw[:, l % 2, :]).then_inc(s["p_hi_done"], 1)
                v.wait_ge(s["p_hi_done"], J * n + l + 1)
                v.tensor_tensor(p_lo[:, l, :], p_raw[:, l % 2, :], p_hi[:, l, :].bitcast(F32), ALU.subtract).then_inc(s["p_lo_done"], 1)

            def finish_x1(n, j):
                v.wait_ge(s["num_mm"], J * n + j + 1)
                v.tensor_tensor(den[:, 0, j:j + 1], xb[j % 2][:, D:D + 1], cnt[:, ds(n, 1), j], ALU.mult).then_inc(s["den_step"], 1)
                v.wait_ge(s["den_step"], 2 * (J * n + j) + 1)
                v.reciprocal(den[:, 1, j:j + 1], den[:, 0, j:j + 1]).then_inc(s["den_step"], 1)
                v.wait_ge(s["den_step"], 2 * (J * n + j) + 2)
                need(v, s["turn_mm"], J * (n - 1) + j + 1)
                v.scalar_tensor_tensor(out=x1n[:, j, :], in0=xb[j % 2][:, 0:D], scalar=den[:, 1, j:j + 1],
                                       in1=xn[:, ds(n & 1, 1), j, :].rearrange("p o d -> p (o d)"), op0=ALU.mult,
                                       op1=ALU.add).then_inc(s["x1_done"], 1)

            def split_lora(n):
                for i, (part, raw) in enumerate(((la, la_raw), (lb, lb_raw))):
                    v.wait_ge(s["lora_hi_done"], 2 * n + i + 1)
                    v.scalar_tensor_tensor(out=part[:, :], in0=raw[:, :], scalar=cf[:, CF_LO + i:CF_LO + i + 1],
                                           in1=part[:, :].bitcast(F32), op0=ALU.mult, op1=ALU.add).then_inc(s["lora_done"], 1)

            def split_x1(n):
                v.wait_ge(s["x1_hi_done"], n + 1)
                need(v, s["l1_mm"], C * n)
                v.tensor_tensor(x1_lo[:, :, :], tb_[:, :, :], x1_hi[:, :, :].bitcast(F32), ALU.subtract).then_inc(s["x1_lo_done"], 1)

            def split_x2(n):
                v.wait_ge(s["x2_done"], n + 1)
                need(v, s["hid_mm"], KF * n)
                v.tensor_scalar(x2_hi[:, :, :], x2[:, ds(n & 1, 1)].rearrange("p o c s -> p (o c) s"), 1.0, None,
                                ALU.mult).then_inc(s["x2_hi_done"], 1)
                v.wait_ge(s["x2_hi_done"], n + 1)
                v.tensor_tensor(x2_lo[:, :, :], x2[:, ds(n & 1, 1)].rearrange("p o c s -> p (o c) s"), x2_hi[:, :, :].bitcast(F32),
                                ALU.subtract).then_inc(s["x2_lo_done"], 1)

            def add_w(n, i):
                v.wait_ge(s["fold_mm"], NFOLD * n + i + 1)
                need(v, s["w_hi_done"], NFOLD * n + i - 1)
                need(v, s["w_lo_done"], NFOLD * n + i - 1)
                v.scalar_tensor_tensor(out=w_sum[:, i % 2, :], in0=tb_[:, i % 2, :], scalar=LORA_ALPHA,
                                       in1=wfold(FOLDS[i], "raw"), op0=ALU.mult, op1=ALU.add).then_inc(s["w_sum_done"], 1)

            def split_hidden(b, k):
                v.wait_ge(s["hid_hi_done"], KF * b + k + 1)
                need(v, s["out_mm"], KF * b + k - 1)
                v.scalar_tensor_tensor(out=hid_lo[:, k % 2, :], in0=rb[k % 2][:, :], scalar=0.0, in1=hid_hi[:, k % 2, :].bitcast(F32),
                                       op0=ALU.max, op1=ALU.subtract).then_inc(s["hid_lo_done"], 1)

            def finish_x3(b):
                v.wait_ge(s["out_mm"], KF * (b + 1))
                need(v, s["lap_mm"], b)
                need(v, s["y_done"], 3 * b)
                need(v, s["lin_done"], b)
                need(v, s["quad_done"], b)
                v.tensor_tensor(x3[:, :, :], ob[:, :, :], x2[:, ds(b & 1, 1)].rearrange("p o c s -> p (o c) s"),
                                ALU.add).then_inc(s["x3_done"], 1)

            def quadratic(b):
                v.wait_ge(s["lin_done"], b + 1)
                v.tensor_tensor(t_quad, t_lin, x3[:, :, :], ALU.mult).then_inc(s["quad_step"], 1)
                v.wait_ge(s["quad_step"], b + 1)
                v.wait_ge(s["lap_mm"], b + 1)
                v.scalar_tensor_tensor(out=t_quad, in0=tb_[:, :, :], scalar=z[:, 0, ds(b, 1)], in1=t_quad, op0=ALU.mult,
                                       op1=ALU.add).then_inc(s["quad_done"], 1)

            def finish_out(b):
                v.wait_ge(s["y_done"], 3 * (b + 1))
                v.wait_ge(s["quad_done"], b + 1)
                need(v, s["stored"], 16 * b)
                v.scalar_tensor_tensor(out=t_out, in0=t_y, scalar=z[:, 1, ds(b, 1)], in1=t_quad, op0=ALU.mult,
                                       op1=ALU.add).then_inc(s["out_done"], 1)

            v.memset(scol[:, :, :], 0.0).then_inc(s["scol_zero"], 1)
            v.wait_ge(s["scol_zero"], 1)
            scores_in(0)
            scores_in(1)
            masks()
            for b in range(2, B):
                scores_in(b)
            row_maxima()
            v.wait_ge(s["ld_wi"], 16)
            v.wait_ge(s["ld_wo"], 16)
            split_lora(0)
            split_h(0)
            for i in range(NFOLD):
                add_w(0, i)
            for l in range(J):
                split_p(0, l)
            for j in range(J):
                finish_x1(0, j)
            split_x1(0)
            split_x2(0)

            def step(b, last=False):
                n = b + 1
                split_hidden(b, 0)
                if not (isinstance(b, int) and b == 0):
                    quadratic(b - 1)
                split_hidden(b, 1)
                if not (isinstance(b, int) and b == 0):
                    finish_out(b - 1)
                if last:
                    for k in range(2, KF):
                        split_hidden(b, k)
                    finish_x3(b)
                    return
                split_p(n, 0)
                split_lora(n)
                split_hidden(b, 2)
                split_p(n, 1)
                split_hidden(b, 3)
                split_p(n, 2)
                split_hidden(b, 4)
                split_p(n, 3)
                split_h(n)
                finish_x1(n, 0)
                finish_x1(n, 1)
                finish_x1(n, 2)
                split_hidden(b, 5)
                finish_x1(n, 3)
                split_hidden(b, 6)
                split_x1(n)
                add_w(n, 0)
                add_w(n, 1)
                split_hidden(b, 7)
                split_x2(n)
                for i in range(2, NFOLD):
                    add_w(n, i)
                finish_x3(b)

            step(0)
            with v.Fori(1, B - 1) as b:
                step(b)
            step(B - 1, last=True)
            quadratic(B - 1)
            finish_out(B - 1)

        @block.gpsimd
        def _(pool):
            def add_residual(n):
                pool.wait_ge(s["ld_wc"], 32 * (n + 1))
                need(pool, s["wc_lo_done"], n)
                need(pool, s["wc_hi_done"], n)
                pool.tensor_tensor(wc_res[:, :, :], wc_raw[:, :, :],
                                   cf[:, CF_RES:CF_RES + C * D].rearrange("p (c d) -> p c d", c=C),
                                   ALU.add).then_inc(s["wc_res_done"], 1)

            def split_wc(n):
                pool.wait_ge(s["wc_hi_done"], n + 1)
                need(pool, s["l1_mm"], C * n)
                pool.tensor_tensor(wc_lo[:, :, :], wc_res[:, :, :], wc_hi[:, :, :].bitcast(F32), ALU.subtract).then_inc(s["wc_lo_done"], 1)

            def split_w(n, i):
                pool.wait_ge(s["w_hi_done"], NFOLD * n + i + 1)
                pool.tensor_tensor(wfold(FOLDS[i], "lo"), w_sum[:, i % 2, :], wfold(FOLDS[i], "hi").bitcast(F32),
                                   ALU.subtract).then_inc(s["w_lo_done"], 1)

            def along_tokens(b):
                pool.wait_ge(s["x3_done"], b + 1)
                need(pool, s["out_done"], b)
                ends = ((0, 1), (S - 1, S - 2))
                for t, at in ends:
                    pool.tensor_tensor(t_y[:, :, t:t + 1], x3[:, :, at:at + 1], x3[:, :, at:at + 1],
                                       ALU.add).then_inc(s["y_done"], 1)
                pool.tensor_tensor(t_y[:, :, 1:S - 1], x3[:, :, 0:S - 2], x3[:, :, 2:S], ALU.add).then_inc(s["y_done"], 1)

            pool.memset(h_lo[:, :, D:ND].bitcast(F32), 0.0).then_inc(s["ones_done"], 1)
            pool.memset(h_hi[:, :, D:ND].bitcast(F32), 1.0).then_inc(s["ones_done"], 1)
            pool.wait_ge(s["ld_cb"], 16)
            pool.tensor_copy(sel[:, :, :], cb[:, CB_HOT:CB_HOT + B * J].rearrange("p (k o) -> p k o", o=1)
                             .broadcast_to([P, B * J, P])).then_inc(s["pool_consts"], 1)
            pool.wait_ge(s["ld_cf"], 16)
            add_residual(0)
            for i in range(NFOLD):
                split_w(0, i)
            split_wc(0)

            def step(b):
                n = b + 1
                if not (isinstance(b, int) and b == 0):
                    along_tokens(b - 1)
                add_residual(n)
                split_wc(n)
                for i in range(NFOLD):
                    split_w(n, i)

            step(0)
            with pool.Fori(1, B - 1) as b:
                step(b)
            along_tokens(B - 2)
            along_tokens(B - 1)


def kernel(**inputs):
    import ml_dtypes
    import numpy as np

    import concourse.bacc as bacc
    from concourse.bass_utils import run_bass_kernel_spmd

    a = {k: np.asarray(v) for k, v in inputs.items()}
    bf16 = ml_dtypes.bfloat16

    def halves(x, axis):
        x = np.moveaxis(x, axis, -1)
        x = np.moveaxis(x.reshape(x.shape[:-1] + (P, C)), -1, -2)
        return np.moveaxis(x, (-2, -1), (axis, axis + 1))

    p, m = np.arange(P)[:, None], np.arange(P)[None, :]
    cf = np.zeros((P, CF_N), np.float32)
    cf[:, CF_ID:CF_ID + P] = p == m
    cf[:, CF_SHIFT:CF_SHIFT + P] = 1 * (p == m) + (p == m - 1)
    cf[0, CF_SHIFT] = 2
    cf[:, CF_SHIFT + P:CF_SHIFT + 2 * P] = 1 * (p == m) + (p == m + 1)
    cf[P - 1, CF_SHIFT + 2 * P - 1] = 2
    for c in range(C):
        cf[:, CF_RES + c * D + c * P:CF_RES + c * D + (c + 1) * P] = p == m
    cf[:, CF_TOK:CF_TOK + J] = np.arange(J)[None, :] * P + p + 1
    for i, low in enumerate((p // Q % 2 == 1, p // Q >= 2)):
        cf[:, CF_LO + i:CF_LO + i + 1] = low
        cf[:, CF_SIGN + i:CF_SIGN + i + 1] = 1 - 2 * low
    cb = np.zeros((P, CB_N), np.float32)
    cb[:, CB_ID:CB_ID + P] = p == m
    cb[:, CB_LO:CB_LO + P] = p > m
    cb[:, CB_UP:CB_UP + P] = p < m
    for b in range(B):
        for l in range(J):
            row = 3 * Q + b * J + l
            blk = np.arange(S) // P
            cb[row, CB_BLO:CB_BLO + S] = l > blk
            cb[row, CB_BUP:CB_BUP + S] = l < blk
            cb[[b, Q + b, 2 * Q + b, row], CB_HOT + b * J + l] = 1
    types = a["itok_B_0_2"]
    typeq = np.zeros((P, 1), types.dtype)
    for q in range(3):
        typeq[q * Q:q * Q + B, 0] = types
    typeq[3 * Q:, 0] = np.repeat(types, J)
    x = a["x"]
    wc = halves(a["L1_cond_W"].reshape(-1, P, C, D), 3)
    arrays = {
        "xT": x.transpose(0, 2, 1).reshape(B, P, C, S),
        "xn": halves(x, 2).reshape(B, J, P, D).transpose(0, 2, 1, 3),
        "cf": cf,
        "cb": cb.astype(bf16),
        "typeq": typeq,
        "types": np.broadcast_to(types, (P, B)),
        "ids": np.concatenate([a["itok_B_0_30"], a["itok_B_0_7"]])[None, :],
        "z": np.broadcast_to(np.stack([a["condB_zX"], a["condB_zY"], a["condB_zR"]]), (P, 3, B)),
        "w1": a["L0_cond_W1"].reshape(P, C, A),
        "b1v": np.stack([a["L0_cond_b1"], a["L0_cond_v"]], axis=1),
        "wc": wc.reshape(-1, P, C, D),
        "bc": a["L1_cond_b"].reshape(-1, P, C),
        "wi": a["L2_cond_wi"].T.reshape(P, C, F),
        "wo": halves(a["L2_cond_wo"].T, 1).reshape(KF, P, D).transpose(1, 0, 2),
        "la_common": np.concatenate([halves(a["L2_cond_common_wi_a"], 1).reshape(-1, D), a["L2_cond_common_wo_a"]], axis=1),
        "la_expert": np.concatenate([halves(a["L2_cond_experts_wi_a"], 2).reshape(NEXP, -1, D), a["L2_cond_experts_wo_a"]], axis=2),
        "lb_common": np.concatenate([a["L2_cond_common_wi_b"].T, halves(a["L2_cond_common_wo_b"].T, 1).reshape(-1, D)], axis=1),
        "lb_expert": np.concatenate([a["L2_cond_experts_wi_b"].transpose(0, 2, 1),
                                     halves(a["L2_cond_experts_wo_b"].transpose(0, 2, 1), 2).reshape(NEXP, -1, D)], axis=2),
    }
    nc = bacc.Bacc("TRN2", target_bir_lowering=False, num_devices=1)
    feed, args = {}, []
    for name, array in arrays.items():
        array = np.ascontiguousarray(array)
        feed[f"{name}_dram"] = array
        args.append(nc.dram_tensor(f"{name}_dram", array.shape, mybir.dt.from_np(array.dtype), kind="ExternalInput").ap())
    out = nc.dram_tensor("out_dram", (B, P, C, S), F32, kind="ExternalOutput").ap()
    build(nc, *args, out)
    got = run_bass_kernel_spmd(nc, [feed], core_ids=[0]).results[0]["out_dram"]
    return np.ascontiguousarray(np.asarray(got).reshape(B, D, S).transpose(0, 2, 1))
```

```python
from contextlib import ExitStack

import concourse.bass as bass
from concourse import mybir

F32 = mybir.dt.float32
F32R = mybir.dt.float32r
BF16 = mybir.dt.bfloat16
I32 = mybir.dt.int32
ALU = mybir.AluOpType
ACT = mybir.ActivationFunctionType
ds = bass.ds

P = 128
B, S, D = 8, 512, 256
A = 64
F = 1024
C = D // P
J = S // P
KF = F // P
LORA_ALPHA = 2.0
RC = 16
ND = D + 2
NCAT, NEXP = 31, 8
XR = 4
Q = 32
NEG = -1e30

CF_ID, CF_TOK = 0, P
CF_LO, CF_SIGN = CF_TOK + J, CF_TOK + J + 2 + 1
CF_CLO, CF_CSIGN, CF_PICK = CF_SIGN + 3, CF_SIGN + 3 + B, CF_SIGN + 3 + 2 * B
CF_N = CF_PICK + J
CB_ID, CB_LO, CB_UP = 0, P, 2 * P
CB_MASK = 3 * P
CB_HOT = CB_MASK + 3 * J
CB_CSEL = CB_HOT + B
CB_N = CB_CSEL + P
GROUPS = [range(0, 2), range(2, B)]
EX = P + 1
WS = 4
EARLY = 6
ALPHA_N = D + F
BETA_N = F + D


def need(eng, sem, value):
    if isinstance(value, int) and value <= 0:
        return
    eng.wait_ge(sem, value)


def build(nc, xT_d, xn_d, cf_d, cb_d, typeq_d, types_d, ids_d, z_d, w1_d, b1v_d, wc_d, bc_d, wi_d, wo_d,
          la_common_d, la_expert_d, lb_common_d, lb_expert_d, out_d):
    with ExitStack() as ctx:
        def sb(name, shape, dt=F32):
            return ctx.enter_context(nc.sbuf_tensor(name, shape, dt))

        def bank(name):
            return ctx.enter_context(nc.psum_tensor(name, [P, S], F32))

        def sem(name):
            return ctx.enter_context(nc.semaphore(name))

        cf = sb("cf", [P, CF_N])
        cb = sb("cb", [P, CB_N], BF16)
        typeq_i = sb("typeq_i", [P, 1], I32)
        types_i = sb("types_i", [P, B], I32)
        ids = sb("ids", [1, 2 * B], I32)
        typeq = sb("typeq", [P, 1])
        types = sb("types", [P, B])
        rowc = sb("rowc", [P, 4])
        rowneg = sb("rowneg", [P, 3])
        batc = sb("batc", [P, 4, B])
        batneg = sb("batneg", [P, 3, B])
        blockneg = sb("blockneg", [P, J])
        cnt_a = sb("cnt_a", [P, B])
        cnt_b = sb("cnt_b", [P, B])
        cnt = sb("cnt", [P, B, J])
        z = sb("z", [P, 3, B])
        zc = sb("zc", [P, 3, B])
        w1 = sb("w1", [P, C, A])
        b1v = sb("b1v", [A, 2])
        sel = sb("sel", [P, B, P], BF16)
        diagmask = sb("diagmask", [P, B, P], BF16)
        diagterm = sb("diagterm", [P, 2, B, P], BF16)
        m3 = [sb(f"m3{g}", [P, S + J], BF16) for g in range(2)]
        scol = [sb(f"scol{g}", [P, J, 3 * Q]) for g in range(2)]
        e_in = sb("e_in", [P, 2, B, J])
        e_all = sb("e_all", [P, 2, B, J])
        lowest = sb("lowest", [P, 1])
        blockmax = sb("blockmax", [P, 2, J])
        maxcol = sb("maxcol", [P, 2, 1])
        maxtmp = sb("maxtmp", [P, J])
        coef = [sb(f"coef{g}", [P, S], F32R) for g in range(2)]
        e4_hi = sb("e4_hi", [P, J * EX], F32R)
        e4_lo = sb("e4_lo", [P, J * EX], F32R)
        cs = sb("cs", [P, ND], F32R)
        scratch = sb("scratch", [P, 4 * C * S])
        tanhT = sb("tanhT", [A, 2, S])
        xn = sb("xn", [P, 2, J, D])
        h_hi = sb("h_hi", [P, J, ND], F32R)
        h_lo = sb("h_lo", [P, J, ND], F32R)
        p_raw = sb("p_raw", [P, 2, S])
        p_hi = sb("p_hi", [P, S], F32R)
        p_lo = sb("p_lo", [P, S], F32R)
        den = sb("den", [P, 2, J])
        x1n = sb("x1n", [P, J, D])
        x1_hi = sb("x1_hi", [P, C, S], F32R)
        x1_lo = sb("x1_lo", [P, C, S], F32R)
        wc_raw = sb("wc_raw", [P, C, D])
        wc_hi = sb("wc_hi", [P, C, D], F32R)
        wc_lo = sb("wc_lo", [P, C, D], F32R)
        bc = sb("bc", [P, 2, C])
        x2 = sb("x2", [P, 2, C, S])
        x2_hi = sb("x2_hi", [P, C, S], F32R)
        x2_lo = sb("x2_lo", [P, C, S], F32R)
        wi = sb("wi", [P, C, F])
        wo = sb("wo", [P, KF, D])
        w_sum = sb("w_sum", [P, WS, S])
        wi_hi = sb("wi_hi", [P, C, F], F32R)
        wi_lo = sb("wi_lo", [P, C, F], F32R)
        wo_hi = sb("wo_hi", [P, KF, D], F32R)
        wo_lo = sb("wo_lo", [P, KF, D], F32R)
        la_raw = sb("la_raw", [P, ALPHA_N])
        lb_raw = sb("lb_raw", [P, BETA_N])
        la = sb("la", [P, ALPHA_N], F32R)
        lb = sb("lb", [P, BETA_N], F32R)
        hid_hi = sb("hid_hi", [P, 2, S], F32R)
        hid_lo = sb("hid_lo", [P, 2, S], F32R)
        x3 = sb("x3", [P, C, S])
        x3_next = sb("x3_next", [P, C, S])

        xT = scratch[:, :].rearrange("p (r c s) -> p r c s", r=XR, c=C)
        t_lin, t_quad, t_y, t_out = (xT[:, i] for i in range(4))
        rowbuf = [x2[:, :, :, :].rearrange("p a c s -> p (a c) s"), scratch[:, 0:4 * S].rearrange("p (a s) -> p a s", a=4)]
        negmax = sb("negmax", [3 * Q, S + J])
        rest = sb("rest", [3 * Q, S + J])
        mid = sb("mid", [3 * Q, S + J], BF16)

        xb = [bank("xb0"), bank("xb1")]
        tb_ = ctx.enter_context(nc.psum_tensor("tb", [P, C, S], F32))
        ob = ctx.enter_context(nc.psum_tensor("ob", [P, C, S], F32))
        rb = [bank("rb0"), bank("rb1")]

        names = """ld_cf ld_cb ld_small ld_w1 ld_wi ld_wo ld_common ld_xn ld_wc ld_lora ld_ids
        proj_mm score_mm turned tanh_done scol_done sel_done m3_done srow_used
        spread_mm e_in_done e_done coef_raw_done coef_hi_done coef_done
        carry_mm logit_mm num_mm turn_mm l1_mm fold_mm hid_mm out_mm
        h_hi_done exp_done c_hi_done x1_hi_done x2_done x2_hi_done hid_hi_done w_hi_done lin_done wc_hi_done
        h_lo_done e4_hi_done e4_lo_done c_done p_hi_done p_lo_done x1_done x1_lo_done x2_lo_done hid_lo_done w_sum_done
        x3_done quad_done out_done dve_step den_step prod_done
        zeros_done e4_zero ones_done lora_hi_done lora_done wc_res_done wc_lo_done w_lo_done srow_step y_done near_done shifted diag_step diag_done types_done stored""".split()
        s = {n: sem(n) for n in names}
        ld_xT = [sem(f"ld_xT{i}") for i in range(XR)]

        block = ctx.enter_context(nc.Block())

        FOLDS = [("wi", 0, 0), ("wi", 1, 0), ("wo", 0), ("wo", 1), ("wi", 0, 1), ("wi", 1, 1), ("wo", 2), ("wo", 3)]
        NFOLD = len(FOLDS)
        fold_at = {f: i for i, f in enumerate(FOLDS)}
        LORA = [(slice(0, D), slice(0, F)), (slice(D, D + F), slice(F, F + D))]

        def group(n):
            return 0 if isinstance(n, int) and n in GROUPS[0] else 1

        def spread(e4):
            return e4[:, :].rearrange("p (j x) -> p j x", x=EX)[:, :, 0:P:J]

        def wfold(f, part):
            if f[0] == "wi":
                return {"raw": wi, "hi": wi_hi, "lo": wi_lo}[part][:, f[1], f[2] * S:(f[2] + 1) * S]
            return {"raw": wo, "hi": wo_hi, "lo": wo_lo}[part][:, 2 * f[1]:2 * f[1] + 2, :].rearrange("p k d -> p (k d)")

        def near_features(eng, b):
            eng.wait_ge(s["shifted"], 4 * 16 * (b + 1))
            for c in range(C):
                eng.tensor_tensor(x3_next[:, c, :], x3_next[:, c, :], x3[:, 1 - c, :], ALU.add).then_inc(s["near_done"], 1)

        def product(eng, b):
            eng.wait_ge(s["lin_done"], b + 1)
            eng.tensor_tensor(t_lin, t_lin, x3[:, :, :], ALU.mult).then_inc(s["prod_done"], 1)

        @block.sync
        def _(sp):
            def load_xT(b):
                if b >= XR:
                    sp.wait_ge(s["proj_mm"], b - XR + 1)
                sp.dma_start(xT[:, b % XR], xT_d[b]).then_inc(ld_xT[b % XR], 16)

            def load_xn(n, slot):
                if not (isinstance(n, int) and n < 2):
                    sp.wait_ge(s["h_hi_done"], n)
                    sp.wait_ge(s["x1_done"], J * (n - 1))
                sp.dma_start(xn[:, ds(slot, 1)], xn_d[ds(n, 1)].rearrange("b p j d -> p b j d")).then_inc(s["ld_xn"], 16)

            def load_wc(n, slot):
                cat = sp.value_load(ids[0:1, ds(n, 1)], min_val=0, max_val=NCAT)
                need(sp, s["x2_done"], C * (n - 1))
                need(sp, s["wc_lo_done"], n)
                sp.dma_start(wc_raw[:, :, :], wc_d[ds(cat, 1)].rearrange("e p c d -> (e p) c d")).then_inc(s["ld_wc"], 16)
                sp.dma_start(bc[:, ds(slot, 1)], bc_d[ds(cat, 1)].rearrange("e p c -> p e c")).then_inc(s["ld_wc"], 16)

            def load_lora(n):
                expert = sp.value_load(ids[0:1, ds(n + B, 1)], min_val=0, max_val=NEXP - 1)
                need(sp, s["lora_done"], 4 * n)
                for raw, expert_d in ((la_raw, la_expert_d), (lb_raw, lb_expert_d)):
                    sp.dma_start(raw[4 * RC:, :], expert_d[ds(expert, 1)].rearrange("e r n -> (e r) n")).then_inc(s["ld_lora"], 16)

            load_xT(0)
            sp.dma_start(w1[:, :, :], w1_d).then_inc(s["ld_w1"], 16)
            sp.dma_start(b1v[:, :], b1v_d).then_inc(s["ld_w1"], 16)
            sp.dma_start(types_i[:, :], types_d).then_inc(s["ld_small"], 16)
            sp.dma_start(typeq_i[:, :], typeq_d).then_inc(s["ld_small"], 16)
            sp.dma_start(cb[:, :], cb_d).then_inc(s["ld_cb"], 16)
            load_xT(1)
            sp.dma_start(cf[:, :], cf_d).then_inc(s["ld_cf"], 16)
            sp.dma_start(z[:, :, :], z_d).then_inc(s["ld_small"], 16)
            sp.dma_start(ids[:, :], ids_d).then_inc(s["ld_ids"], 16)
            load_xT(2)
            load_xT(3)
            load_xn(0, 0)
            load_xT(4)
            for raw, common_d in ((la_raw, la_common_d), (lb_raw, lb_common_d)):
                sp.dma_start(raw[0:4 * RC, :], common_d).then_inc(s["ld_common"], 16)
            sp.wait_ge(s["ld_ids"], 16)
            load_lora(0)
            load_xT(5)
            sp.dma_start(wi[:, :, :], wi_d).then_inc(s["ld_wi"], 16)
            sp.dma_start(wo[:, :, :], wo_d).then_inc(s["ld_wo"], 16)
            load_wc(0, 0)
            load_xT(6)
            load_xT(7)
            sp.wait_ge(s["ld_xn"], 16)
            load_xn(1, 1)

            def shift(b):
                sp.wait_ge(s["x3_done"], b + 1)
                for half, to, at in ((0, slice(1, P), slice(0, P - 1)), (0, slice(0, 1), slice(0, 1)),
                                     (1, slice(0, P - 1), slice(1, P)), (1, slice(P - 1, P), slice(P - 1, P))):
                    sp.dma_start(x3_next[to, half, :], x3[at, 1 - half, :]).then_inc(s["shifted"], 16)

            def store(n):
                sp.wait_ge(s["out_done"], n + 1)
                sp.dma_start(out_d[ds(n, 1)].rearrange("b p c s -> (b p) c s"), t_out).then_inc(s["stored"], 16)

            def step(b, l3=True, xn_left=True):
                slot = b & 1
                load_lora(b + 1)
                if l3:
                    shift(b - 1)
                load_wc(b + 1, 1 - slot)
                if xn_left:
                    load_xn(b + 2, slot)
                if l3:
                    store(b - 1)

            step(0, l3=False)
            with sp.Fori(1, B - 2) as b:
                step(b)
            step(B - 2, xn_left=False)
            shift(B - 2)
            store(B - 2)
            shift(B - 1)
            store(B - 1)
            sp.wait_ge(s["stored"], 16 * B)

        @block.tensor
        def _(pe):
            def split_matmul(out, w_hi, w_lo, x_hi, x_lo, first, last):
                pe.matmul(out, w_hi, x_hi, start=first, stop=False)
                pe.matmul(out, w_hi, x_lo, start=False, stop=False)
                return pe.matmul(out, w_lo, x_hi, start=False, stop=last)

            def project(b):
                pe.wait_ge(ld_xT[b % XR], 16 * (b // XR + 1))
                if b >= 2:
                    pe.wait_ge(s["scol_done"], b - 1)
                for c in range(C):
                    mm = pe.matmul(rb[b % 2][0:A, :], w1[:, c, :], xT[:, b % XR, c, :], start=c == 0, stop=c == C - 1)
                mm.then_inc(s["proj_mm"], 1)

            def score(b):
                pe.wait_ge(s["tanh_done"], b + 1)
                for j in range(J):
                    mm = pe.matmul(rb[b % 2][:, j:j + 1], tanhT[:, b % 2, j * P:(j + 1) * P], b1v[:, 1:2],
                                   start=True, stop=True)
                mm.then_inc(s["score_mm"], 1)

            def score_rows(g):
                pe.wait_ge(s["scol_done"], GROUPS[g].stop)
                if g:
                    pe.wait_ge(s["w_sum_done"], EARLY)
                for j in range(J):
                    mm = pe.transpose(tb_[0:3 * Q, 0, j * P:(j + 1) * P], scol[g][:, j, :], cf[:, CF_ID:CF_ID + P])
                mm.then_inc(s["turned"], 1)

            def spread_maxima(g):
                pe.wait_ge(s["m3_done"], g + 1)
                if g:
                    pe.wait_ge(s["x2_done"], C * 2)
                else:
                    pe.wait_ge(s["sel_done"], 1)
                blocks = m3[g][:, S:S + J]
                for b in GROUPS[g]:
                    pe.matmul(xb[1][:, b * J:(b + 1) * J], sel[:, b, :], blocks, start=True, stop=True)
                pe.matmul(xb[1][:, B * J:(B + 1) * J], cb[:, CB_CSEL:CB_CSEL + P], blocks, start=True, stop=True)
                pe.matmul(xb[0][:, :], cb[:, CB_CSEL:CB_CSEL + P], m3[g][:, 0:S], start=True, stop=True)\
                    .then_inc(s["spread_mm"], 1)

            def carry_sums(n):
                need(pe, s["x2_done"], C * n)
                if isinstance(n, int) and n == 0:
                    pe.wait_ge(s["ones_done"], 2)
                if isinstance(n, int) and n in (0, 2):
                    pe.wait_ge(s["coef_raw_done"], group(n) + 1)
                pe.wait_ge(s["e4_lo_done"], n + 1)
                pe.wait_ge(s["h_hi_done"], n + 1)
                pe.wait_ge(s["h_lo_done"], n + 1)
                for j in range(J):
                    cols = slice(j * P, (j + 1) * P)
                    mm = split_matmul(xb[0][:, 0:ND], e4_hi[:, cols], e4_lo[:, cols], h_hi[:, j, :], h_lo[:, j, :],
                                      j == 0, j == J - 1)
                mm.then_inc(s["carry_mm"], 1)

            def logits(n):
                need(pe, s["x2_done"], C * n)
                if isinstance(n, int) and n in (0, 2):
                    pe.wait_ge(s["e_in_done"], group(n) + 1)
                if isinstance(n, int) and n == 0:
                    pe.wait_ge(s["diag_done"], 1)
                pe.matmul(xb[1][:, :], sel[:, ds(n, 1), :].rearrange("p o m -> p (o m)"), m3[group(n)][:, 0:S],
                          start=True, stop=False)
                pe.matmul(xb[1][:, :], cb[:, CB_ID:CB_ID + P], diagmask[:, ds(n, 1), :].broadcast_to([P, J, P]),
                          start=False, stop=True).then_inc(s["logit_mm"], 1)

            def pool_block(n, j):
                if j == 0:
                    pe.wait_ge(s["c_done"], n + 1)
                    pe.wait_ge(s["p_lo_done"], n + 1)
                    if isinstance(n, int) and n in (0, 2):
                        pe.wait_ge(s["coef_done"], group(n) + 1)
                elif j == 1:
                    pe.wait_ge(s["exp_done"], J * n + J)
                else:
                    pe.wait_ge(s["x1_done"], J * n + j - 1)
                cols = slice(j * P, (j + 1) * P)
                split_matmul(xb[j % 2][:, 0:ND], p_hi[:, cols], p_lo[:, cols], h_hi[:, j, :], h_lo[:, j, :], True, False)
                pe.matmul(xb[j % 2][:, 0:ND], coef[group(n)][:, cols], cs[:, :], start=False, stop=True)\
                    .then_inc(s["num_mm"], 1)

            def turn(n, j):
                pe.wait_ge(s["x1_done"], J * n + j + 1)
                if j == 0:
                    pe.wait_ge(s["w_sum_done"], 2 if isinstance(n, int) and n == 0 else NFOLD * n + NFOLD // 2)
                for c in range(C):
                    mm = pe.transpose(tb_[:, c, j * P:(j + 1) * P], x1n[:, j, c * P:(c + 1) * P], cf[:, CF_ID:CF_ID + P])
                mm.then_inc(s["turn_mm"], 1)

            def layer1(n):
                pe.wait_ge(s["x1_hi_done"], n + 1)
                pe.wait_ge(s["x1_lo_done"], n + 1)
                pe.wait_ge(s["wc_hi_done"], n + 1)
                pe.wait_ge(s["wc_lo_done"], n + 1)
                for co in range(C):
                    for c in range(C):
                        cols = slice(co * P, (co + 1) * P)
                        mm = split_matmul(xb[co][:, :], wc_hi[:, c, cols], wc_lo[:, c, cols], x1_hi[:, c, :], x1_lo[:, c, :],
                                          c == 0, c == C - 1)
                    mm.then_inc(s["l1_mm"], 1)

            def fold(n, f):
                i = fold_at[f]
                if i in (0, 2):
                    pe.wait_ge(s["lora_done"], 4 * n + i + 2)
                first = isinstance(n, int) and n == 0
                if i in ((2, 3) if first else (NFOLD // 2, NFOLD // 2 + 1)):
                    pe.wait_ge(s["x1_lo_done"], n + 1)
                elif first and i < 2:
                    pe.wait_ge(s["srow_used"], 1)
                else:
                    pe.wait_ge(s["w_sum_done"], NFOLD * n + i - 1)
                    if first and i == EARLY:
                        pe.wait_ge(s["srow_used"], 2)
                if f[0] == "wi":
                    mm = pe.matmul(tb_[:, i % 2, :], la[:, f[1] * P:(f[1] + 1) * P], lb[:, f[2] * S:(f[2] + 1) * S],
                                   start=True, stop=True)
                else:
                    for k in range(2):
                        kf = 2 * f[1] + k
                        mm = pe.matmul(tb_[:, i % 2, k * D:(k + 1) * D], la[:, D + kf * P:D + (kf + 1) * P], lb[:, F:F + D],
                                       start=True, stop=True)
                mm.then_inc(s["fold_mm"], 1)

            def hidden(b, k):
                if isinstance(b, int) and b == 0 and k < 2:
                    pe.wait_ge(s["scol_done"], B - 1 + k)
                if k == 0:
                    pe.wait_ge(s["x2_hi_done"], C * (b + 1))
                    pe.wait_ge(s["x2_lo_done"], C * (b + 1))
                if k % (KF // 2) == 0:
                    ready = NFOLD * b + fold_at[("wi", 1, k // (KF // 2))] + 1
                    pe.wait_ge(s["w_hi_done"], ready)
                    pe.wait_ge(s["w_lo_done"], ready)
                need(pe, s["hid_lo_done"], KF * b + k - 1)
                for c in range(C):
                    cols = slice(k * P, (k + 1) * P)
                    mm = split_matmul(rb[k % 2][:, :], wi_hi[:, c, cols], wi_lo[:, c, cols], x2_hi[:, c, :], x2_lo[:, c, :],
                                      c == 0, c == C - 1)
                mm.then_inc(s["hid_mm"], 1)

            def output(b, k):
                if k == 0:
                    need(pe, s["x3_done"], b)
                if k % 2 == 0:
                    ready = NFOLD * b + fold_at[("wo", k // 2)] + 1
                    pe.wait_ge(s["w_hi_done"], ready)
                    pe.wait_ge(s["w_lo_done"], ready)
                pe.wait_ge(s["hid_hi_done"], KF * b + k + 1)
                pe.wait_ge(s["hid_lo_done"], KF * b + k + 1)
                for c in range(C):
                    cols = slice(c * P, (c + 1) * P)
                    mm = split_matmul(ob[:, c, :], wo_hi[:, k, cols], wo_lo[:, k, cols], hid_hi[:, k % 2, :],
                                      hid_lo[:, k % 2, :], k == 0, k == KF - 1)
                mm.then_inc(s["out_mm"], 1)

            pe.wait_ge(s["ld_w1"], 32)
            project(0)
            project(1)
            score(0)
            score(1)
            pe.wait_ge(s["ld_cf"], 16)
            score_rows(0)
            project(2)
            project(3)
            score(2)
            score(3)
            spread_maxima(0)
            project(4)
            carry_sums(0)
            logits(0)
            fold(0, FOLDS[0])
            fold(0, FOLDS[1])
            score(4)
            project(5)
            for j in range(J):
                pool_block(0, j)
            score(5)
            for j in range(J):
                turn(0, j)
            project(6)
            layer1(0)
            fold(0, FOLDS[2])
            fold(0, FOLDS[3])
            score(6)
            project(7)
            fold(0, FOLDS[4])
            fold(0, FOLDS[5])

            def step(b):
                n = b + 1
                hidden(b, 0)
                if isinstance(b, int) and b == 0:
                    score(7)
                    score_rows(1)
                hidden(b, 1)
                fold(b, FOLDS[6])
                fold(b, FOLDS[7])
                carry_sums(n)
                logits(n)
                output(b, 0)
                hidden(b, 2)
                output(b, 1)
                hidden(b, 3)
                output(b, 2)
                fold(n, FOLDS[0])
                fold(n, FOLDS[1])
                hidden(b, 4)
                pool_block(n, 0)
                pool_block(n, 1)
                output(b, 3)
                fold(n, FOLDS[2])
                fold(n, FOLDS[3])
                pool_block(n, 2)
                hidden(b, 5)
                pool_block(n, 3)
                output(b, 4)
                for j in range(J):
                    turn(n, j)
                hidden(b, 6)
                output(b, 5)
                hidden(b, 7)
                layer1(n)
                fold(n, FOLDS[4])
                fold(n, FOLDS[5])
                output(b, 6)
                output(b, 7)
                if isinstance(b, int) and b == 0:
                    spread_maxima(1)

            step(0)
            step(1)
            with pe.Fori(2, B - 1) as b:
                step(b)
            hidden(B - 1, 0)
            hidden(B - 1, 1)
            fold(B - 1, FOLDS[6])
            fold(B - 1, FOLDS[7])
            output(B - 1, 0)
            for k in range(2, KF):
                hidden(B - 1, k)
                output(B - 1, k - 1)
            output(B - 1, KF - 1)

        @block.scalar
        def _(act):
            def split_h(n):
                act.wait_ge(s["ld_xn"], 16 * (n + 1))
                need(act, s["num_mm"], J * n)
                act.activation(h_hi[:, :, 0:D], xn[:, ds(n & 1, 1)].rearrange("p o j d -> p (o j) d"),
                               ACT.Copy).then_inc(s["h_hi_done"], 1)

            def exps(n):
                act.wait_ge(s["logit_mm"], n + 1)
                need(act, s["p_lo_done"], n)
                for l in range(J):
                    act.activation(p_raw[:, 0, l * P:(l + 1) * P], xb[1][:, l * P:(l + 1) * P], ACT.Exp,
                                   bias=scol[group(n)][:, l, ds(n, 1)]).then_inc(s["exp_done"], 1)

            def round_carry(n):
                act.wait_ge(s["carry_mm"], n + 1)
                need(act, s["num_mm"], J * n)
                act.activation(cs[:, :], xb[0][:, 0:ND], ACT.Copy,
                               scale=cf[:, ds(n + CF_CSIGN, 1)]).then_inc(s["c_hi_done"], 1)

            def spread_exps(g):
                act.wait_ge(s["e_in_done"], g + 1)
                bs = GROUPS[g]
                act.activation(e_all[:, g, bs.start:bs.stop], e_in[:, g, bs.start:bs.stop], ACT.Exp).then_inc(s["e_done"], 1)
                act.activation(p_raw[:, 1, :], xb[0][:, :], ACT.Exp, bias=maxcol[:, g]).then_inc(s["coef_raw_done"], 1)
                act.wait_ge(s["coef_raw_done"], g + 1)
                act.activation(coef[g][:, :], p_raw[:, 1, :], ACT.Copy,
                               scale=cf[:, CF_SIGN + 2:CF_SIGN + 3]).then_inc(s["coef_hi_done"], 1)

            def split_x1(n):
                act.wait_ge(s["turn_mm"], J * (n + 1))
                need(act, s["l1_mm"], C * n)
                act.activation(x1_hi[:, :, :], tb_[:, :, :], ACT.Copy).then_inc(s["x1_hi_done"], 1)

            def bias_x2(n):
                need(act, s["x3_done"], n - 1)
                for c in range(C):
                    act.wait_ge(s["l1_mm"], C * n + c + 1)
                    act.activation(x2[:, ds(n & 1, 1), c, :].rearrange("p o s -> p (o s)"), xb[c][:, :], ACT.Identity,
                                   bias=bc[:, ds(n & 1, 1), c]).then_inc(s["x2_done"], 1)

            def split_wc(n):
                act.wait_ge(s["wc_res_done"], 2 * (n + 1))
                need(act, s["l1_mm"], C * n)
                act.activation(wc_hi[:, :, :], wc_raw[:, :, :], ACT.Copy).then_inc(s["wc_hi_done"], 1)

            def round_lora(n, g):
                if g == 0:
                    act.wait_ge(s["ld_lora"], 2 * 16 * (n + 1))
                need(act, s["fold_mm"], NFOLD * n - 2 + 2 * g)
                for i, cols in enumerate(LORA[g]):
                    part, raw = ((la, la_raw), (lb, lb_raw))[i]
                    act.activation(part[:, cols], raw[:, cols], ACT.Copy,
                                   scale=cf[:, CF_SIGN + i:CF_SIGN + i + 1]).then_inc(s["lora_hi_done"], 1)

            def relu_hidden(b, k):
                act.wait_ge(s["hid_mm"], KF * b + k + 1)
                need(act, s["out_mm"], KF * b + k - 1)
                act.activation(hid_hi[:, k % 2, :], rb[k % 2][:, :], ACT.Relu).then_inc(s["hid_hi_done"], 1)

            def split_w(n, i):
                act.wait_ge(s["w_sum_done"], NFOLD * n + i + 1)
                used = KF * n - (KF // 2 if i < NFOLD // 2 else 0)
                need(act, s["hid_mm"] if FOLDS[i][0] == "wi" else s["out_mm"], used)
                act.activation(wfold(FOLDS[i], "hi"), w_sum[:, i % WS, :], ACT.Copy).then_inc(s["w_hi_done"], 1)

            def linear(b):
                act.wait_ge(s["x3_done"], b + 1)
                need(act, s["quad_done"], b)
                if isinstance(b, int) and b == 0:
                    act.wait_ge(s["m3_done"], 2)
                act.activation(t_lin, x3[:, :, :], ACT.Identity, bias=zc[:, 1, ds(b, 1)],
                               scale=zc[:, 2, ds(b, 1)]).then_inc(s["lin_done"], 1)

            def tanh(b):
                act.wait_ge(s["proj_mm"], b + 1)
                if b >= 2:
                    act.wait_ge(s["score_mm"], b - 1)
                act.activation(tanhT[:, b % 2, :], rb[b % 2][0:A, :], ACT.Tanh, bias=b1v[:, 0:1]).then_inc(s["tanh_done"], 1)

            act.wait_ge(s["ld_w1"], 32)
            tanh(0)
            tanh(1)
            split_h(0)
            act.wait_ge(s["ld_cf"], 16)
            tanh(2)
            tanh(3)
            act.wait_ge(s["ld_common"], 2 * 16)
            round_lora(0, 0)
            round_lora(0, 1)
            spread_exps(0)
            tanh(4)
            round_carry(0)
            exps(0)
            tanh(5)
            split_w(0, 0)
            split_w(0, 1)
            split_wc(0)
            split_x1(0)
            tanh(6)
            bias_x2(0)
            split_w(0, 2)
            split_w(0, 3)
            tanh(7)
            split_w(0, 4)
            split_w(0, 5)
            split_h(1)

            def step(b, last=False, h_left=True):
                n = b + 1
                first = isinstance(b, int) and b == 0
                relu_hidden(b, 0)
                relu_hidden(b, 1)
                if not first:
                    linear(b - 1)
                split_w(b, 6)
                split_w(b, 7)
                if last:
                    for k in range(2, KF):
                        relu_hidden(b, k)
                    return
                round_carry(n)
                exps(n)
                relu_hidden(b, 2)
                round_lora(n, 0)
                relu_hidden(b, 3)
                round_lora(n, 1)
                relu_hidden(b, 4)
                split_w(n, 0)
                split_w(n, 1)
                split_wc(n)
                relu_hidden(b, 5)
                split_w(n, 2)
                split_w(n, 3)
                split_x1(n)
                relu_hidden(b, 6)
                if h_left:
                    split_h(n + 1)
                relu_hidden(b, 7)
                bias_x2(n)
                split_w(n, 4)
                split_w(n, 5)
                if first:
                    spread_exps(1)

            step(0)
            step(1)
            with act.Fori(2, B - 2) as b:
                step(b)
            step(B - 2, h_left=False)
            step(B - 1, last=True)
            linear(B - 1)

        @block.vector
        def _(v):
            steps = [0]

            def link(ins):
                ins.then_inc(s["dve_step"], 1)
                steps[0] += 1
                v.wait_ge(s["dve_step"], steps[0])

            def scores_in(b):
                g = group(b)
                v.wait_ge(s["score_mm"], b + 1)
                src = rb[b % 2][:, 0:J].rearrange("p (j o) -> p j o", o=1).broadcast_to([P, J, 3])
                v.tensor_copy(scol[g][:, :, b:b + 2 * Q + 1:Q], src).then_inc(s["scol_done"], 1)

            def types_masks():
                v.wait_ge(s["ld_small"], 48)
                link(v.tensor_copy(types[:, :], types_i[:, :]))
                for col in range(2):
                    link(v.tensor_scalar(batc[:, col], types[:, :], float(col), None, ALU.is_equal))
                link(v.tensor_tensor(batc[:, 3], batc[:, 0], batc[:, 1], ALU.add))
                link(v.tensor_scalar(batc[:, 2], batc[:, 3], -1.0, 1.0, ALU.mult, ALU.add))
                v.tensor_scalar(batneg[:, :, :], batc[:, 0:3], NEG, None, ALU.mult).then_inc(s["types_done"], 1)
                link(v.tensor_copy(typeq[:, :], typeq_i[:, :]))
                for col in range(2):
                    link(v.tensor_scalar(rowc[:, col:col + 1], typeq[:, :], float(col), None, ALU.is_equal))
                link(v.tensor_tensor(rowc[:, 3:4], rowc[:, 0:1], rowc[:, 1:2], ALU.add))
                link(v.tensor_scalar(rowc[:, 2:3], rowc[:, 3:4], -1.0, 1.0, ALU.mult, ALU.add))
                link(v.tensor_scalar(rowneg[:, :], rowc[:, 0:3], NEG, None, ALU.mult))
                link(v.tensor_scalar(rowc[:, 0:3], rowc[:, 0:3], -1.0, None, ALU.mult))
                v.wait_ge(s["ld_cb"], 16)
                link(v.tensor_scalar(blockneg[:, :], cb[:, CB_MASK:CB_MASK + J], rowneg[:, 0:1], None, ALU.mult))
                for t in (1, 2):
                    link(v.scalar_tensor_tensor(out=blockneg[:, :], in0=cb[:, CB_MASK + t * J:CB_MASK + (t + 1) * J],
                                                scalar=rowneg[:, t:t + 1], in1=blockneg[:, :], op0=ALU.mult, op1=ALU.add))
                q3 = slice(3 * Q, 4 * Q)
                for g in range(2):
                    link(v.tensor_copy(m3[g][q3, 0:S].rearrange("p (j t) -> p j t", j=J),
                                       blockneg[q3, :].rearrange("p (j o) -> p j o", o=1).broadcast_to([Q, J, P])))
                    link(v.memset(m3[g][q3, S:S + J], 0.0))

            def counts():
                v.wait_ge(s["ld_cf"], 16)
                link(v.tensor_tensor(cnt_a[:, :], batc[:, 0], batc[:, 1], ALU.subtract))
                link(v.tensor_scalar(cnt_b[:, :], batc[:, 1], float(S + 1), None, ALU.mult))
                link(v.scalar_tensor_tensor(out=cnt_b[:, :], in0=batc[:, 2], scalar=float(S - 1), in1=cnt_b[:, :],
                                            op0=ALU.mult, op1=ALU.add))
                for j in range(J):
                    link(v.scalar_tensor_tensor(out=cnt[:, :, j], in0=cnt_a[:, :], scalar=cf[:, CF_TOK + j:CF_TOK + j + 1],
                                                in1=cnt_b[:, :], op0=ALU.mult, op1=ALU.add))

            def reaction():
                link(v.tensor_tensor(zc[:, 0], z[:, 0], z[:, 1], ALU.add))
                link(v.tensor_scalar(zc[:, 1], zc[:, 0], -2.0, 1.0, ALU.mult, ALU.add))
                link(v.tensor_tensor(zc[:, 1], zc[:, 1], z[:, 2], ALU.add))
                link(v.tensor_scalar(zc[:, 2], z[:, 2], -1.0, None, ALU.mult))

            rows = slice(0, 3 * Q)

            def row_maxima(g):
                premax, postmax = (rowbuf[g][rows, i, :] for i in range(2))
                srow = tb_[rows, 0, :]
                floor = lowest[rows, :].broadcast_to([3 * Q, S])
                v.wait_ge(s["turned"], g + 1)
                v.tensor_tensor_scan(premax, srow, floor, -3e38, ALU.max, ALU.max).then_inc(s["srow_step"], 1)
                v.tensor_tensor_scan(postmax[:, ::-1], srow[:, ::-1], floor, -3e38, ALU.max, ALU.max)\
                    .then_inc(s["srow_step"], 1)
                v.tensor_reduce(blockmax[rows, g, :], srow.rearrange("p (j t) -> p j t", j=J), mybir.AxisListType.X,
                                ALU.max).then_inc(s["srow_used"], 1)
                v.wait_ge(s["srow_step"], 2 * (g + 1))
                v.wait_ge(s["srow_used"], g + 1)
                link(v.tensor_scalar(negmax[:, S:S + J], blockmax[rows, g, :], -1.0, None, ALU.mult))

            def pick_maxima(g):
                premax, postmax, exmax = (rowbuf[g][rows, i, :] for i in range(3))
                link(v.tensor_tensor(exmax[:, 1:S - 1], premax[:, 0:S - 2], postmax[:, 2:S], ALU.max))
                link(v.tensor_copy(exmax[:, 0:1], postmax[:, 1:2]))
                link(v.tensor_copy(exmax[:, S - 1:S], premax[:, S - 2:S - 1]))
                out = negmax[:, 0:S]
                link(v.tensor_scalar(out, premax, rowc[rows, 0:1], None, ALU.mult))
                link(v.scalar_tensor_tensor(out=out, in0=postmax, scalar=rowc[rows, 1:2], in1=out, op0=ALU.mult, op1=ALU.add))
                link(v.scalar_tensor_tensor(out=out, in0=exmax, scalar=rowc[rows, 2:3], in1=out, op0=ALU.mult, op1=ALU.add))

            def part_maxima(g):
                link(v.tensor_copy(m3[g][rows, :], negmax[:, :]))
                link(v.tensor_tensor(rest[:, :], negmax[:, :], m3[g][rows, :], ALU.subtract))
                link(v.tensor_copy(mid[:, :], rest[:, :]))
                link(v.tensor_tensor(rest[:, :], rest[:, :], mid[:, :], ALU.subtract))
                link(v.tensor_copy(m3[g][Q:2 * Q, :], mid[Q:2 * Q, :]))
                v.tensor_copy(m3[g][2 * Q:3 * Q, :], rest[2 * Q:3 * Q, :]).then_inc(s["m3_done"], 1)

            def spread_in(g):
                bs = GROUPS[g]
                v.wait_ge(s["spread_mm"], g + 1)
                link(v.tensor_tensor(maxtmp[:, :], xb[1][:, B * J:(B + 1) * J], cf[:, CF_PICK:CF_PICK + J], ALU.mult))
                link(v.tensor_reduce(maxcol[:, g], maxtmp[:, :], mybir.AxisListType.X, ALU.add))
                v.tensor_tensor(e_in[:, g, bs.start:bs.stop], xb[1][:, bs.start * J:bs.stop * J].rearrange("p (b j) -> p b j", j=J),
                                scol[g][:, :, bs.start:bs.stop].rearrange("p j b -> p b j"), ALU.add).then_inc(s["e_in_done"], 1)

            def split_coef(g):
                v.wait_ge(s["coef_hi_done"], g + 1)
                v.scalar_tensor_tensor(out=coef[g][:, :], in0=p_raw[:, 1, :], scalar=cf[:, CF_LO + 2:CF_LO + 3],
                                       in1=coef[g][:, :].bitcast(F32), op0=ALU.mult, op1=ALU.add).then_inc(s["coef_done"], 1)

            def spread_e(n):
                if isinstance(n, int) and n in (0, 2):
                    v.wait_ge(s["e_done"], group(n) + 1)
                    v.wait_ge(s["e4_zero"], 2)
                need(v, s["carry_mm"], n)
                e = e_all[:, group(n), ds(n, 1), :].rearrange("p o j -> p (o j)").rearrange("p (j o) -> p j o", o=1)\
                    .broadcast_to([P, J, Q])
                v.tensor_scalar(spread(e4_hi), e, 1.0, None, ALU.mult).then_inc(s["e4_hi_done"], 1)
                v.wait_ge(s["e4_hi_done"], n + 1)
                v.tensor_tensor(spread(e4_lo), e, spread(e4_hi).bitcast(F32), ALU.subtract).then_inc(s["e4_lo_done"], 1)

            def split_carry(n):
                v.wait_ge(s["c_hi_done"], n + 1)
                v.scalar_tensor_tensor(out=cs[:, :], in0=xb[0][:, 0:ND], scalar=cf[:, ds(n + CF_CLO, 1)],
                                       in1=cs[:, :].bitcast(F32), op0=ALU.mult, op1=ALU.add).then_inc(s["c_done"], 1)

            def split_p(n):
                v.wait_ge(s["exp_done"], J * (n + 1))
                need(v, s["num_mm"], J * n)
                v.tensor_copy(p_hi[:, :], p_raw[:, 0, :]).then_inc(s["p_hi_done"], 1)
                v.wait_ge(s["p_hi_done"], n + 1)
                v.tensor_tensor(p_lo[:, :], p_raw[:, 0, :], p_hi[:, :].bitcast(F32), ALU.subtract).then_inc(s["p_lo_done"], 1)

            def finish_x1(n, j):
                v.wait_ge(s["num_mm"], J * n + j + 1)
                v.tensor_tensor(den[:, 0, j:j + 1], xb[j % 2][:, D:D + 1], cnt[:, ds(n, 1), j], ALU.mult).then_inc(s["den_step"], 1)
                v.wait_ge(s["den_step"], 2 * (J * n + j) + 1)
                v.reciprocal(den[:, 1, j:j + 1], den[:, 0, j:j + 1]).then_inc(s["den_step"], 1)
                v.wait_ge(s["den_step"], 2 * (J * n + j) + 2)
                need(v, s["turn_mm"], J * (n - 1) + j + 1)
                v.scalar_tensor_tensor(out=x1n[:, j, :], in0=xb[j % 2][:, 0:D], scalar=den[:, 1, j:j + 1],
                                       in1=xn[:, ds(n & 1, 1), j, :].rearrange("p o d -> p (o d)"), op0=ALU.mult,
                                       op1=ALU.add).then_inc(s["x1_done"], 1)

            def split_lora(n, g):
                for i, cols in enumerate(LORA[g]):
                    part, raw = ((la, la_raw), (lb, lb_raw))[i]
                    v.wait_ge(s["lora_hi_done"], 4 * n + 2 * g + i + 1)
                    v.scalar_tensor_tensor(out=part[:, cols], in0=raw[:, cols], scalar=cf[:, CF_LO + i:CF_LO + i + 1],
                                           in1=part[:, cols].bitcast(F32), op0=ALU.mult, op1=ALU.add).then_inc(s["lora_done"], 1)

            def split_x1(n):
                v.wait_ge(s["x1_hi_done"], n + 1)
                need(v, s["l1_mm"], C * n)
                v.tensor_tensor(x1_lo[:, :, :], tb_[:, :, :], x1_hi[:, :, :].bitcast(F32), ALU.subtract).then_inc(s["x1_lo_done"], 1)

            def split_x2(n):
                need(v, s["hid_mm"], KF * n)
                for c in range(C):
                    x2_c = x2[:, ds(n & 1, 1), c, :].rearrange("p o s -> p (o s)")
                    v.wait_ge(s["x2_done"], C * n + c + 1)
                    v.tensor_scalar(x2_hi[:, c, :], x2_c, 1.0, None, ALU.mult).then_inc(s["x2_hi_done"], 1)
                    v.wait_ge(s["x2_hi_done"], C * n + c + 1)
                    v.tensor_tensor(x2_lo[:, c, :], x2_c, x2_hi[:, c, :].bitcast(F32), ALU.subtract).then_inc(s["x2_lo_done"], 1)

            def add_w(n, i):
                v.wait_ge(s["fold_mm"], NFOLD * n + i + 1)
                need(v, s["w_hi_done"], NFOLD * n + i - WS + 1)
                need(v, s["w_lo_done"], NFOLD * n + i - WS + 1)
                v.scalar_tensor_tensor(out=w_sum[:, i % WS, :], in0=tb_[:, i % 2, :], scalar=LORA_ALPHA,
                                       in1=wfold(FOLDS[i], "raw"), op0=ALU.mult, op1=ALU.add).then_inc(s["w_sum_done"], 1)

            def split_hidden(b, k):
                v.wait_ge(s["hid_hi_done"], KF * b + k + 1)
                need(v, s["out_mm"], KF * b + k - 1)
                v.scalar_tensor_tensor(out=hid_lo[:, k % 2, :], in0=rb[k % 2][:, :], scalar=0.0, in1=hid_hi[:, k % 2, :].bitcast(F32),
                                       op0=ALU.max, op1=ALU.subtract).then_inc(s["hid_lo_done"], 1)

            def finish_x3(b):
                v.wait_ge(s["out_mm"], KF * (b + 1))
                need(v, s["lin_done"], b)
                need(v, s["y_done"], 3 * b)
                need(v, s["prod_done"], b)
                need(v, s["near_done"], C * b)
                need(v, s["quad_done"], b)
                v.tensor_tensor(x3[:, :, :], ob[:, :, :], x2[:, ds(b & 1, 1)].rearrange("p o c s -> p (o c) s"),
                                ALU.add).then_inc(s["x3_done"], 1)

            def quadratic(b):
                v.wait_ge(s["prod_done"], b + 1)
                v.wait_ge(s["near_done"], C * (b + 1))
                need(v, s["out_done"], b)
                v.scalar_tensor_tensor(out=t_quad, in0=x3_next[:, :, :], scalar=z[:, 0, ds(b, 1)], in1=t_lin, op0=ALU.mult,
                                       op1=ALU.add).then_inc(s["quad_done"], 1)

            def finish_out(b):
                v.wait_ge(s["y_done"], 3 * (b + 1))
                v.wait_ge(s["quad_done"], b + 1)
                need(v, s["stored"], 16 * b)
                v.scalar_tensor_tensor(out=t_out, in0=t_y, scalar=z[:, 1, ds(b, 1)], in1=t_quad, op0=ALU.mult,
                                       op1=ALU.add).then_inc(s["out_done"], 1)

            v.memset(scol[0][:, :, :], 0.0).then_inc(s["zeros_done"], 1)
            v.memset(scol[1][:, :, :], 0.0).then_inc(s["zeros_done"], 1)
            v.memset(lowest[:, :], -3e38).then_inc(s["zeros_done"], 1)
            types_masks()
            v.wait_ge(s["zeros_done"], 3)
            scores_in(0)
            scores_in(1)
            row_maxima(0)
            pick_maxima(0)
            part_maxima(0)
            scores_in(2)
            scores_in(3)
            spread_in(0)
            spread_e(0)
            counts()
            split_coef(0)
            split_lora(0, 0)
            split_carry(0)
            v.wait_ge(s["ld_wi"], 16)
            add_w(0, 0)
            split_p(0)
            scores_in(4)
            add_w(0, 1)
            for j in range(J):
                finish_x1(0, j)
            scores_in(5)
            split_lora(0, 1)
            split_x1(0)
            reaction()
            spread_e(1)
            scores_in(6)
            split_x2(0)
            v.wait_ge(s["ld_wo"], 16)
            add_w(0, 2)
            add_w(0, 3)
            add_w(0, 4)
            add_w(0, 5)
            scores_in(7)

            def step(b, last=False, e_left=True):
                n = b + 1
                first = isinstance(b, int) and b == 0
                split_hidden(b, 0)
                if first:
                    row_maxima(1)
                split_hidden(b, 1)
                add_w(b, 6)
                add_w(b, 7)
                if last:
                    for k in range(2, KF):
                        split_hidden(b, k)
                        if k == 4:
                            quadratic(b - 1)
                        if k == 5:
                            finish_out(b - 1)
                    finish_x3(b)
                    return
                split_carry(n)
                split_p(n)
                split_hidden(b, 2)
                split_lora(n, 0)
                split_hidden(b, 3)
                split_lora(n, 1)
                add_w(n, 0)
                add_w(n, 1)
                finish_x1(n, 0)
                split_hidden(b, 4)
                finish_x1(n, 1)
                add_w(n, 2)
                add_w(n, 3)
                finish_x1(n, 2)
                finish_x1(n, 3)
                split_hidden(b, 5)
                if first:
                    pick_maxima(1)
                else:
                    quadratic(b - 1)
                split_x1(n)
                split_hidden(b, 6)
                split_hidden(b, 7)
                if first:
                    part_maxima(1)
                else:
                    finish_out(b - 1)
                split_x2(n)
                add_w(n, 4)
                add_w(n, 5)
                if e_left and not first:
                    spread_e(n + 1)
                finish_x3(b)
                if first:
                    spread_in(1)
                    spread_e(n + 1)
                    split_coef(1)

            step(0)
            step(1)
            with v.Fori(2, B - 2) as b:
                step(b)
            step(B - 2, e_left=False)
            step(B - 1, last=True)
            product(v, B - 1)
            near_features(v, B - 1)
            quadratic(B - 1)
            finish_out(B - 1)

        @block.gpsimd
        def _(pool):
            def add_residual(n):
                pool.wait_ge(s["ld_wc"], 32 * (n + 1))
                for c in range(C):
                    diag = wc_raw[:, c, c * P:(c + 1) * P]
                    pool.tensor_tensor(diag, diag, cf[:, CF_ID:CF_ID + P], ALU.add).then_inc(s["wc_res_done"], 1)

            def split_wc(n):
                pool.wait_ge(s["wc_hi_done"], n + 1)
                need(pool, s["l1_mm"], C * n)
                pool.tensor_tensor(wc_lo[:, :, :], wc_raw[:, :, :], wc_hi[:, :, :].bitcast(F32), ALU.subtract).then_inc(s["wc_lo_done"], 1)

            def split_w(n, i):
                pool.wait_ge(s["w_hi_done"], NFOLD * n + i + 1)
                pool.tensor_tensor(wfold(FOLDS[i], "lo"), w_sum[:, i % WS, :], wfold(FOLDS[i], "hi").bitcast(F32),
                                   ALU.subtract).then_inc(s["w_lo_done"], 1)

            def along_tokens(b):
                pool.wait_ge(s["x3_done"], b + 1)
                need(pool, s["out_done"], b)
                ends = ((0, 1), (S - 1, S - 2))
                for t, at in ends:
                    pool.tensor_tensor(t_y[:, :, t:t + 1], x3[:, :, at:at + 1], x3[:, :, at:at + 1],
                                       ALU.add).then_inc(s["y_done"], 1)
                pool.tensor_tensor(t_y[:, :, 1:S - 1], x3[:, :, 0:S - 2], x3[:, :, 2:S], ALU.add).then_inc(s["y_done"], 1)

            def split_h(n):
                pool.wait_ge(s["h_hi_done"], n + 1)
                need(pool, s["num_mm"], J * n)
                pool.tensor_tensor(h_lo[:, :, 0:D], xn[:, ds(n & 1, 1)].rearrange("p o j d -> p (o j) d"),
                                   h_hi[:, :, 0:D].bitcast(F32), ALU.subtract).then_inc(s["h_lo_done"], 1)

            def diagonal_masks():
                pool.wait_ge(s["types_done"], 1)
                terms = (diagmask[:, :, :], diagterm[:, 0], diagterm[:, 1])
                for t, col in enumerate((CB_LO, CB_UP, CB_ID)):
                    pool.tensor_tensor(terms[t], cb[:, col:col + P].rearrange("p (o m) -> p o m", o=1).broadcast_to([P, B, P]),
                                       batneg[:, t].rearrange("p (b o) -> p b o", o=1).broadcast_to([P, B, P]),
                                       ALU.mult).then_inc(s["diag_step"], 1)
                pool.wait_ge(s["diag_step"], 3)
                pool.tensor_tensor(diagmask[:, :, :], diagmask[:, :, :], terms[1], ALU.add).then_inc(s["diag_step"], 1)
                pool.wait_ge(s["diag_step"], 4)
                pool.tensor_tensor(diagmask[:, :, :], diagmask[:, :, :], terms[2], ALU.add).then_inc(s["diag_done"], 1)

            pool.memset(h_lo[:, :, D:ND].bitcast(F32), 0.0).then_inc(s["ones_done"], 1)
            pool.memset(h_hi[:, :, D:ND].bitcast(F32), 1.0).then_inc(s["ones_done"], 1)
            pool.memset(e4_hi[:, :].bitcast(F32), 0.0).then_inc(s["e4_zero"], 1)
            pool.memset(e4_lo[:, :].bitcast(F32), 0.0).then_inc(s["e4_zero"], 1)
            pool.wait_ge(s["ld_cb"], 16)
            pool.tensor_copy(sel[:, :, :], cb[:, CB_HOT:CB_HOT + B].rearrange("p (k o) -> p k o", o=1)
                             .broadcast_to([P, B, P])).then_inc(s["sel_done"], 1)
            diagonal_masks()
            split_h(0)
            split_w(0, 0)
            split_w(0, 1)
            pool.wait_ge(s["ld_cf"], 16)
            add_residual(0)
            split_wc(0)
            for i in range(2, EARLY):
                split_w(0, i)
            split_h(1)

            def step(b, last=False, h_left=True):
                n = b + 1
                for i in range(EARLY, NFOLD):
                    split_w(b, i)
                if not (isinstance(b, int) and b == 0):
                    product(pool, b - 1)
                    along_tokens(b - 1)
                if not last:
                    add_residual(n)
                if not (isinstance(b, int) and b == 0):
                    near_features(pool, b - 1)
                if last:
                    return
                split_w(n, 0)
                split_w(n, 1)
                split_wc(n)
                split_w(n, 2)
                split_w(n, 3)
                if h_left:
                    split_h(n + 1)
                for i in range(NFOLD // 2, EARLY):
                    split_w(n, i)

            step(0)
            step(1)
            with pool.Fori(2, B - 2) as b:
                step(b)
            step(B - 2, h_left=False)
            step(B - 1, last=True)
            along_tokens(B - 1)


def kernel(**inputs):
    import ml_dtypes
    import numpy as np

    import concourse.bacc as bacc
    from concourse.bass_utils import run_bass_kernel_spmd

    a = {k: np.asarray(v) for k, v in inputs.items()}
    bf16 = ml_dtypes.bfloat16

    def halves(x, axis):
        x = np.moveaxis(x, axis, -1)
        x = np.moveaxis(x.reshape(x.shape[:-1] + (P, C)), -1, -2)
        return np.moveaxis(x, (-2, -1), (axis, axis + 1))

    p, m = np.arange(P)[:, None], np.arange(P)[None, :]
    cf = np.zeros((P, CF_N), np.float32)
    cf[:, CF_ID:CF_ID + P] = p == m
    cf[:, CF_TOK:CF_TOK + J] = np.arange(J)[None, :] * P + p + 1
    copy = p // RC % 4
    for i, low in enumerate((copy % 2 == 1, copy >= 2, p // Q >= 2)):
        cf[:, CF_LO + i:CF_LO + i + 1] = low
        cf[:, CF_SIGN + i:CF_SIGN + i + 1] = 1 - 2 * low
    cb = np.zeros((P, CB_N), np.float32)
    cb[:, CB_ID:CB_ID + P] = p == m
    cb[:, CB_LO:CB_LO + P] = p > m
    cb[:, CB_UP:CB_UP + P] = p < m
    blk = np.arange(J)
    for b in range(B):
        cb[[b, Q + b, 2 * Q + b], CB_HOT + b] = 1
        for l in range(J):
            row = 3 * Q + b * J + l
            for t, masked in enumerate((l >= blk, l <= blk, l == blk)):
                cb[row, CB_MASK + t * J:CB_MASK + (t + 1) * J] = masked
            for q in range(4):
                cb[[b, Q + b, 2 * Q + b, row], CB_CSEL + q * Q + b * J + l] = 1
    for b in range(B):
        own = p % Q // J == b
        cf[:, CF_CLO + b:CF_CLO + b + 1] = own * (p // Q % 2 == 1)
        cf[:, CF_CSIGN + b:CF_CSIGN + b + 1] = own * (1 - 2 * (p // Q % 2 == 1))
    cf[:, CF_PICK:CF_PICK + J] = -1.0 * (p % J == np.arange(J)[None, :])
    types = a["itok_B_0_2"]
    typeq = np.zeros((P, 1), types.dtype)
    for q in range(3):
        typeq[q * Q:q * Q + B, 0] = types
    typeq[3 * Q:, 0] = np.repeat(types, J)
    x = a["x"]
    wc = halves(a["L1_cond_W"].reshape(-1, P, C, D), 3)
    arrays = {
        "xT": x.transpose(0, 2, 1).reshape(B, P, C, S),
        "xn": halves(x, 2).reshape(B, J, P, D).transpose(0, 2, 1, 3),
        "cf": cf,
        "cb": cb.astype(bf16),
        "typeq": typeq,
        "types": np.broadcast_to(types, (P, B)),
        "ids": np.concatenate([a["itok_B_0_30"], a["itok_B_0_7"]])[None, :],
        "z": np.broadcast_to(np.stack([a["condB_zX"], a["condB_zY"], a["condB_zR"]]), (P, 3, B)),
        "w1": a["L0_cond_W1"].reshape(P, C, A),
        "b1v": np.stack([a["L0_cond_b1"], a["L0_cond_v"]], axis=1),
        "wc": wc.reshape(-1, P, C, D),
        "bc": a["L1_cond_b"].reshape(-1, P, C),
        "wi": a["L2_cond_wi"].T.reshape(P, C, F),
        "wo": halves(a["L2_cond_wo"].T, 1).reshape(KF, P, D).transpose(1, 0, 2),
        "la_common": np.concatenate([halves(a["L2_cond_common_wi_a"], 1).reshape(-1, D), a["L2_cond_common_wo_a"]], axis=1),
        "la_expert": np.concatenate([halves(a["L2_cond_experts_wi_a"], 2).reshape(NEXP, -1, D), a["L2_cond_experts_wo_a"]], axis=2),
        "lb_common": np.concatenate([a["L2_cond_common_wi_b"].T, halves(a["L2_cond_common_wo_b"].T, 1).reshape(-1, D)], axis=1),
        "lb_expert": np.concatenate([a["L2_cond_experts_wi_b"].transpose(0, 2, 1),
                                     halves(a["L2_cond_experts_wo_b"].transpose(0, 2, 1), 2).reshape(NEXP, -1, D)], axis=2),
    }
    for name in ("la_common", "lb_common"):
        arrays[name] = np.tile(arrays[name], (4, 1))
    for name in ("la_expert", "lb_expert"):
        arrays[name] = np.tile(arrays[name], (1, 4, 1))
    nc = bacc.Bacc("TRN2", target_bir_lowering=False, num_devices=1)
    feed, args = {}, []
    for name, array in arrays.items():
        array = np.ascontiguousarray(array)
        feed[f"{name}_dram"] = array
        args.append(nc.dram_tensor(f"{name}_dram", array.shape, mybir.dt.from_np(array.dtype), kind="ExternalInput").ap())
    out = nc.dram_tensor("out_dram", (B, P, C, S), F32, kind="ExternalOutput").ap()
    build(nc, *args, out)
    got = run_bass_kernel_spmd(nc, [feed], core_ids=[0]).results[0]["out_dram"]
    return np.ascontiguousarray(np.asarray(got).reshape(B, D, S).transpose(0, 2, 1))
```

```python
from contextlib import ExitStack

import concourse.bass as bass
from concourse import mybir

F32 = mybir.dt.float32
F32R = mybir.dt.float32r
BF16 = mybir.dt.bfloat16
I32 = mybir.dt.int32
ALU = mybir.AluOpType
ACT = mybir.ActivationFunctionType
ds = bass.ds

P = 128
B, S, D = 8, 512, 256
A = 64
F = 1024
C = D // P
J = S // P
KF = F // P
LORA_ALPHA = 2.0
RC = 16
ND = D + 2
NCAT, NEXP = 31, 8
XR = 4
Q = 32
NEG = -1e30

CF_ID, CF_TOK = 0, P
CF_LO, CF_SIGN = CF_TOK + J, CF_TOK + J + 2 + 1
CF_CLO, CF_CSIGN, CF_PICK = CF_SIGN + 3, CF_SIGN + 3 + B, CF_SIGN + 3 + 2 * B
CF_N = CF_PICK + J
CB_ID, CB_LO, CB_UP = 0, P, 2 * P
CB_MASK = 3 * P
CB_HOT = CB_MASK + 3 * J
CB_CSEL = CB_HOT + B
CB_N = CB_CSEL + P
GROUPS = [range(0, 2), range(2, B)]
EX = P + 1
WS = 4
EARLY = 6
ALPHA_N = D + F
BETA_N = F + D


def need(eng, sem, value):
    if isinstance(value, int) and value <= 0:
        return
    eng.wait_ge(sem, value)


def build(nc, xT_d, xn_d, cf_d, cb_d, typeq_d, types_d, ids_d, z_d, w1_d, b1v_d, wc_d, bc_d, wi_d, wo_d,
          la_common_d, la_expert_d, lb_common_d, lb_expert_d, out_d):
    with ExitStack() as ctx:
        def sb(name, shape, dt=F32):
            return ctx.enter_context(nc.sbuf_tensor(name, shape, dt))

        def bank(name):
            return ctx.enter_context(nc.psum_tensor(name, [P, S], F32))

        def sem(name):
            return ctx.enter_context(nc.semaphore(name))

        cf = sb("cf", [P, CF_N])
        cb = sb("cb", [P, CB_N], BF16)
        typeq_i = sb("typeq_i", [P, 1], I32)
        types_i = sb("types_i", [P, B], I32)
        ids = sb("ids", [1, 2 * B], I32)
        typeq = sb("typeq", [P, 1])
        types = sb("types", [P, B])
        rowc = sb("rowc", [P, 4])
        rowneg = sb("rowneg", [P, 3])
        batc = sb("batc", [P, 4, B])
        batneg = sb("batneg", [P, 3, B])
        blockneg = sb("blockneg", [P, J])
        cnt_a = sb("cnt_a", [P, B])
        cnt_b = sb("cnt_b", [P, B])
        cnt = sb("cnt", [P, B, J])
        z = sb("z", [P, 3, B])
        zc = sb("zc", [P, 3, B])
        w1 = sb("w1", [P, C, A])
        b1v = sb("b1v", [A, 2])
        sel = sb("sel", [P, B, P], BF16)
        diagmask = sb("diagmask", [P, B, P], BF16)
        diagterm = sb("diagterm", [P, 2, B, P], BF16)
        m3 = [sb(f"m3{g}", [P, S + J], BF16) for g in range(2)]
        scol = [sb(f"scol{g}", [P, J, 3 * Q]) for g in range(2)]
        e_in = sb("e_in", [P, 2, B, J])
        e_all = sb("e_all", [P, 2, B, J])
        zeros = sb("zeros", [P, S], BF16)
        tanh_warm = sb("tanh_warm", [P, 1])
        sel_f = sb("sel_f", [P, 3, P])
        lowest = sb("lowest", [P, 1])
        blockmax = sb("blockmax", [P, 2, J])
        maxcol = sb("maxcol", [P, 2, 1])
        maxtmp = sb("maxtmp", [P, J])
        coef = [sb(f"coef{g}", [P, S], F32R) for g in range(2)]
        e4_hi = sb("e4_hi", [P, J * EX], F32R)
        e4_lo = sb("e4_lo", [P, J * EX], F32R)
        cs = sb("cs", [P, ND], F32R)
        scratch = sb("scratch", [P, 4 * C * S])
        tanhT = sb("tanhT", [A, 2, S])
        xn = sb("xn", [P, 2, J, D])
        h_hi = sb("h_hi", [P, J, ND], F32R)
        h_lo = sb("h_lo", [P, J, ND], F32R)
        p_raw = sb("p_raw", [P, 2, S])
        p_hi = sb("p_hi", [P, S], F32R)
        p_lo = sb("p_lo", [P, S], F32R)
        den = sb("den", [P, 2, J])
        x1n = sb("x1n", [P, J, D])
        x1_hi = sb("x1_hi", [P, C, S], F32R)
        x1_lo = sb("x1_lo", [P, C, S], F32R)
        wc_raw = sb("wc_raw", [P, C, D])
        wc_hi = sb("wc_hi", [P, C, D], F32R)
        wc_lo = sb("wc_lo", [P, C, D], F32R)
        bc = sb("bc", [P, 2, C])
        x2 = sb("x2", [P, 2, C, S])
        x2_hi = sb("x2_hi", [P, C, S], F32R)
        x2_lo = sb("x2_lo", [P, C, S], F32R)
        wi = sb("wi", [P, C, F])
        wo = sb("wo", [P, KF, D])
        w_sum = sb("w_sum", [P, WS, S])
        wi_hi = sb("wi_hi", [P, C, F], F32R)
        wi_lo = sb("wi_lo", [P, C, F], F32R)
        wo_hi = sb("wo_hi", [P, KF, D], F32R)
        wo_lo = sb("wo_lo", [P, KF, D], F32R)
        la_raw = sb("la_raw", [P, ALPHA_N])
        lb_raw = sb("lb_raw", [P, BETA_N])
        la = sb("la", [P, ALPHA_N], F32R)
        lb = sb("lb", [P, BETA_N], F32R)
        hid_hi = sb("hid_hi", [P, 2, S], F32R)
        hid_lo = sb("hid_lo", [P, 2, S], F32R)
        x3 = sb("x3", [P, C, S])
        x3_next = sb("x3_next", [P, C, S])

        xT = scratch[:, :].rearrange("p (r c s) -> p r c s", r=XR, c=C)
        t_lin, t_quad, t_y, t_out = (xT[:, i] for i in range(4))
        rowbuf = [x2[:, :, :, :].rearrange("p a c s -> p (a c) s"), scratch[:, 0:4 * S].rearrange("p (a s) -> p a s", a=4)]
        negmax = sb("negmax", [P, S + J])
        rest = sb("rest", [3 * Q, S + J])
        mid = sb("mid", [3 * Q, S + J], BF16)

        xb = [bank("xb0"), bank("xb1")]
        tb_ = ctx.enter_context(nc.psum_tensor("tb", [P, C, S], F32))
        ob = ctx.enter_context(nc.psum_tensor("ob", [P, C, S], F32))
        rb = [bank("rb0"), bank("rb1")]

        names = """ld_cf ld_cb ld_types ld_z ld_w1 ld_wi ld_wo ld_common ld_xn ld_wc ld_lora ld_ids
        proj_mm score_mm turned tanh_done scol_done sel_done m3_done srow_used
        spread_mm e_in_done e_done coef_raw_done coef_hi_done coef_done
        carry_mm logit_mm num_mm turn_mm l1_mm fold_mm hid_mm out_mm
        h_hi_done exp_done c_hi_done x1_hi_done x2_done x2_hi_done hid_hi_done w_hi_done lin_done wc_hi_done
        h_lo_done e4_hi_done e4_lo_done c_done p_hi_done p_lo_done x1_done x1_lo_done x2_lo_done hid_lo_done w_sum_done
        x3_done quad_done out_done dve_step den_step prod_done
        zeros_done warm_zero end_out end_x3 end_lin end_y end_stored e4_zero ones_done lora_hi_done lora_done
        wc_res_done wc_lo_done w_lo_done srow_step pick_started mid_done mid_placed negmax_done sel_f_done
        row_types y_done near_done shifted diag_step diag_done types_done stored""".split()
        s = {n: sem(n) for n in names}
        end_shifted = [sem(f"end_shifted{c}") for c in range(C)]
        ld_xT = [sem(f"ld_xT{i}") for i in range(XR)]

        block = ctx.enter_context(nc.Block())

        FOLDS = [("wi", 0, 0), ("wi", 1, 0), ("wo", 0), ("wo", 1), ("wi", 0, 1), ("wi", 1, 1), ("wo", 2), ("wo", 3)]
        NFOLD = len(FOLDS)
        fold_at = {f: i for i, f in enumerate(FOLDS)}
        LORA = [(slice(0, D), slice(0, F)), (slice(D, D + F), slice(F, F + D))]

        def group(n):
            return 0 if isinstance(n, int) and n in GROUPS[0] else 1

        def score_bank(g):
            return ob[:, 1, :] if g else tb_[:, 0, :]

        def spread(e4):
            return e4[:, :].rearrange("p (j x) -> p j x", x=EX)[:, :, 0:P:J]

        def wfold(f, part):
            if f[0] == "wi":
                return {"raw": wi, "hi": wi_hi, "lo": wi_lo}[part][:, f[1], f[2] * S:(f[2] + 1) * S]
            return {"raw": wo, "hi": wo_hi, "lo": wo_lo}[part][:, 2 * f[1]:2 * f[1] + 2, :].rearrange("p k d -> p (k d)")

        def near_features(eng, b):
            eng.wait_ge(s["shifted"], 4 * 16 * (b + 1))
            for c in range(C):
                eng.tensor_tensor(x3_next[:, c, :], x3_next[:, c, :], x3[:, 1 - c, :], ALU.add).then_inc(s["near_done"], 1)

        def product(eng, b):
            eng.wait_ge(s["lin_done"], b + 1)
            eng.tensor_tensor(t_lin, t_lin, x3[:, :, :], ALU.mult).then_inc(s["prod_done"], 1)

        @block.sync
        def _(sp):
            def load_xT(b):
                if b >= XR:
                    sp.wait_ge(s["proj_mm"], b - XR + 1)
                sp.dma_start(xT[:, b % XR], xT_d[b]).then_inc(ld_xT[b % XR], 16)

            def load_xn(n, slot):
                if not (isinstance(n, int) and n < 2):
                    sp.wait_ge(s["h_hi_done"], n)
                    sp.wait_ge(s["x1_done"], J * (n - 1))
                sp.dma_start(xn[:, ds(slot, 1)], xn_d[ds(n, 1)].rearrange("b p j d -> p b j d")).then_inc(s["ld_xn"], 16)

            def load_wc(n, slot):
                cat = sp.value_load(ids[0:1, ds(n, 1)], min_val=0, max_val=NCAT)
                need(sp, s["x2_done"], C * (n - 1))
                need(sp, s["wc_lo_done"], n)
                sp.dma_start(wc_raw[:, :, :], wc_d[ds(cat, 1)].rearrange("e p c d -> (e p) c d")).then_inc(s["ld_wc"], 16)
                sp.dma_start(bc[:, ds(slot, 1)], bc_d[ds(cat, 1)].rearrange("e p c -> p e c")).then_inc(s["ld_wc"], 16)

            def load_lora(n):
                expert = sp.value_load(ids[0:1, ds(n + B, 1)], min_val=0, max_val=NEXP - 1)
                need(sp, s["lora_done"], 4 * n)
                for raw, expert_d in ((la_raw, la_expert_d), (lb_raw, lb_expert_d)):
                    sp.dma_start(raw[4 * RC:, :], expert_d[ds(expert, 1)].rearrange("e r n -> (e r) n")).then_inc(s["ld_lora"], 16)

            load_xT(0)
            sp.dma_start(w1[:, :, :], w1_d).then_inc(s["ld_w1"], 16)
            sp.dma_start(b1v[:, :], b1v_d).then_inc(s["ld_w1"], 16)
            sp.dma_start(types_i[:, :], types_d).then_inc(s["ld_types"], 16)
            sp.dma_start(typeq_i[:, :], typeq_d).then_inc(s["ld_types"], 16)
            sp.dma_start(cb[:, :], cb_d).then_inc(s["ld_cb"], 16)
            sp.dma_start(cf[:, :], cf_d).then_inc(s["ld_cf"], 16)
            load_xT(1)
            sp.dma_start(z[:, :, :], z_d).then_inc(s["ld_z"], 16)
            sp.dma_start(ids[:, :], ids_d).then_inc(s["ld_ids"], 16)
            load_xT(2)
            load_xT(3)
            load_xn(0, 0)
            load_xT(4)
            for raw, common_d in ((la_raw, la_common_d), (lb_raw, lb_common_d)):
                sp.dma_start(raw[0:4 * RC, :], common_d).then_inc(s["ld_common"], 16)
            sp.wait_ge(s["ld_ids"], 16)
            load_lora(0)
            load_xT(5)
            sp.dma_start(wi[:, :, :], wi_d).then_inc(s["ld_wi"], 16)
            sp.dma_start(wo[:, :, :], wo_d).then_inc(s["ld_wo"], 16)
            load_wc(0, 0)
            load_xT(6)
            load_xT(7)
            sp.wait_ge(s["ld_xn"], 16)
            load_xn(1, 1)

            def shifts(half):
                return (((slice(1, P), slice(0, P - 1)), (slice(0, 1), slice(0, 1))) if half == 0 else
                        ((slice(0, P - 1), slice(1, P)), (slice(P - 1, P), slice(P - 1, P))))

            def shift(b):
                sp.wait_ge(s["x3_done"], b + 1)
                for half in range(C):
                    for to, at in shifts(half):
                        sp.dma_start(x3_next[to, half, :], x3[at, 1 - half, :]).then_inc(s["shifted"], 16)

            def store(n):
                sp.wait_ge(s["out_done"], n + 1)
                sp.dma_start(out_d[ds(n, 1)].rearrange("b p c s -> (b p) c s"), t_out).then_inc(s["stored"], 16)

            def step(b, l3=True, xn_left=True):
                slot = b & 1
                load_lora(b + 1)
                if l3:
                    shift(b - 1)
                load_wc(b + 1, 1 - slot)
                if xn_left:
                    load_xn(b + 2, slot)
                if l3:
                    store(b - 1)

            step(0, l3=False)
            with sp.Fori(1, B - 2) as b:
                step(b)
            step(B - 2, xn_left=False)
            shift(B - 2)
            store(B - 2)
            for c in range(C):
                sp.wait_ge(s["end_x3"], c + 1)
                for to, at in shifts(1 - c):
                    sp.dma_start(x3_next[to, 1 - c, :], x3[at, c, :]).then_inc(end_shifted[1 - c], 16)
            for i, c in enumerate((1, 0)):
                sp.wait_ge(s["out_done"], B + i)
                sp.dma_start(out_d[B - 1, :, c, :], t_out[:, c, :]).then_inc(s["end_stored"], 16)
            sp.wait_ge(s["stored"], 16 * (B - 1))
            sp.wait_ge(s["end_stored"], 16 * C)

        @block.tensor
        def _(pe):
            def split_matmul(out, w_hi, w_lo, x_hi, x_lo, first, last):
                pe.matmul(out, w_hi, x_hi, start=first, stop=False)
                pe.matmul(out, w_hi, x_lo, start=False, stop=False)
                return pe.matmul(out, w_lo, x_hi, start=False, stop=last)

            def project(b):
                pe.wait_ge(ld_xT[b % XR], 16 * (b // XR + 1))
                if b >= 2:
                    pe.wait_ge(s["scol_done"], b - 1)
                for c in range(C):
                    mm = pe.matmul(rb[b % 2][0:A, :], w1[:, c, :], xT[:, b % XR, c, :], start=c == 0, stop=c == C - 1)
                mm.then_inc(s["proj_mm"], 1)

            def score(b):
                pe.wait_ge(s["tanh_done"], b + 1)
                for j in range(J):
                    mm = pe.matmul(rb[b % 2][:, j:j + 1], tanhT[:, b % 2, j * P:(j + 1) * P], b1v[:, 1:2],
                                   start=True, stop=True)
                mm.then_inc(s["score_mm"], 1)

            def score_rows(g):
                pe.wait_ge(s["scol_done"], GROUPS[g].stop)
                for j in range(J):
                    mm = pe.transpose(score_bank(g)[0:3 * Q, j * P:(j + 1) * P], scol[g][:, j, :], cf[:, CF_ID:CF_ID + P])
                mm.then_inc(s["turned"], 1)

            def spread_maxima(g):
                if g == 0:
                    pe.wait_ge(s["negmax_done"], 1)
                    pe.wait_ge(s["sel_f_done"], 4)
                    blocks = negmax[:, S:S + J]
                    for b in GROUPS[0]:
                        pe.matmul(xb[1][:, b * J:(b + 1) * J], sel_f[:, b, :], blocks, start=True, stop=True)
                    pe.matmul(xb[1][:, B * J:(B + 1) * J], sel_f[:, 2, :], blocks, start=True, stop=True)
                    pe.matmul(xb[0][:, :], sel_f[:, 2, :], negmax[:, 0:S], start=True, stop=True).then_inc(s["spread_mm"], 1)
                    return
                pe.wait_ge(s["m3_done"], g + 1)
                pe.wait_ge(s["mid_placed"], g + 1)
                pe.wait_ge(s["sel_done"], 2)
                pe.wait_ge(s["x2_done"], C * 2)
                blocks = m3[g][:, S:S + J]
                for b in GROUPS[g]:
                    pe.matmul(xb[1][:, b * J:(b + 1) * J], sel[:, b, :], blocks, start=True, stop=True)
                pe.matmul(xb[1][:, B * J:(B + 1) * J], cb[:, CB_CSEL:CB_CSEL + P], blocks, start=True, stop=True)
                pe.matmul(xb[0][:, :], cb[:, CB_CSEL:CB_CSEL + P], m3[g][:, 0:S], start=True, stop=True)\
                    .then_inc(s["spread_mm"], 1)

            def carry_sums(n):
                need(pe, s["x2_done"], C * n)
                if isinstance(n, int) and n == 0:
                    pe.wait_ge(s["ones_done"], 2)
                if isinstance(n, int) and n in (0, 2):
                    pe.wait_ge(s["coef_raw_done"], group(n) + 1)
                pe.wait_ge(s["e4_lo_done"], n + 1)
                pe.wait_ge(s["h_hi_done"], n + 1)
                pe.wait_ge(s["h_lo_done"], n + 1)
                for j in range(J):
                    cols = slice(j * P, (j + 1) * P)
                    mm = split_matmul(xb[0][:, 0:ND], e4_hi[:, cols], e4_lo[:, cols], h_hi[:, j, :], h_lo[:, j, :],
                                      j == 0, j == J - 1)
                mm.then_inc(s["carry_mm"], 1)

            def logits(n):
                need(pe, s["x2_done"], C * n)
                if isinstance(n, int) and n in (0, 2):
                    pe.wait_ge(s["e_in_done"], group(n) + 1)
                    pe.wait_ge(s["sel_done"], group(n) + 1)
                    pe.wait_ge(s["diag_done"], group(n) + 1)
                if isinstance(n, int) and n == 0:
                    pe.wait_ge(s["m3_done"], 1)
                    pe.wait_ge(s["mid_placed"], 1)
                pe.matmul(xb[1][:, :], sel[:, ds(n, 1), :].rearrange("p o m -> p (o m)"), m3[group(n)][:, 0:S],
                          start=True, stop=False)
                pe.matmul(xb[1][:, :], cb[:, CB_ID:CB_ID + P], diagmask[:, ds(n, 1), :].broadcast_to([P, J, P]),
                          start=False, stop=True).then_inc(s["logit_mm"], 1)

            def pool_block(n, j):
                if j == 0:
                    pe.wait_ge(s["c_done"], n + 1)
                    pe.wait_ge(s["p_lo_done"], n + 1)
                    if isinstance(n, int) and n in (0, 2):
                        pe.wait_ge(s["coef_done"], group(n) + 1)
                elif j == 1:
                    pe.wait_ge(s["exp_done"], J * n + J)
                else:
                    pe.wait_ge(s["x1_done"], J * n + j - 1)
                cols = slice(j * P, (j + 1) * P)
                split_matmul(xb[j % 2][:, 0:ND], p_hi[:, cols], p_lo[:, cols], h_hi[:, j, :], h_lo[:, j, :], True, False)
                pe.matmul(xb[j % 2][:, 0:ND], coef[group(n)][:, cols], cs[:, :], start=False, stop=True)\
                    .then_inc(s["num_mm"], 1)

            def turn(n, j):
                pe.wait_ge(s["x1_done"], J * n + j + 1)
                if j == 0 and isinstance(n, int) and n == 0:
                    pe.wait_ge(s["srow_used"], 1)
                elif j == 0:
                    pe.wait_ge(s["w_sum_done"], NFOLD * n + NFOLD // 2)
                for c in range(C):
                    mm = pe.transpose(tb_[:, c, j * P:(j + 1) * P], x1n[:, j, c * P:(c + 1) * P], cf[:, CF_ID:CF_ID + P])
                mm.then_inc(s["turn_mm"], 1)

            def layer1(n):
                pe.wait_ge(s["x1_hi_done"], n + 1)
                pe.wait_ge(s["x1_lo_done"], n + 1)
                pe.wait_ge(s["wc_hi_done"], n + 1)
                pe.wait_ge(s["wc_lo_done"], n + 1)
                for co in range(C):
                    for c in range(C):
                        cols = slice(co * P, (co + 1) * P)
                        mm = split_matmul(xb[co][:, :], wc_hi[:, c, cols], wc_lo[:, c, cols], x1_hi[:, c, :], x1_lo[:, c, :],
                                          c == 0, c == C - 1)
                    mm.then_inc(s["l1_mm"], 1)

            def fold(n, f):
                i = fold_at[f]
                if i in (0, 2):
                    pe.wait_ge(s["lora_done"], 4 * n + i + 2)
                first = isinstance(n, int) and n == 0
                if i in ((0, 1) if first else (NFOLD // 2, NFOLD // 2 + 1)):
                    pe.wait_ge(s["x1_lo_done"], n + 1)
                else:
                    pe.wait_ge(s["w_sum_done"], NFOLD * n + i - 1)
                if f[0] == "wi":
                    mm = pe.matmul(tb_[:, i % 2, :], la[:, f[1] * P:(f[1] + 1) * P], lb[:, f[2] * S:(f[2] + 1) * S],
                                   start=True, stop=True)
                else:
                    for k in range(2):
                        kf = 2 * f[1] + k
                        mm = pe.matmul(tb_[:, i % 2, k * D:(k + 1) * D], la[:, D + kf * P:D + (kf + 1) * P], lb[:, F:F + D],
                                       start=True, stop=True)
                mm.then_inc(s["fold_mm"], 1)

            def hidden(b, k):
                if isinstance(b, int) and b == 0 and k < 2:
                    pe.wait_ge(s["scol_done"], B - 1 + k)
                if k == 0:
                    pe.wait_ge(s["x2_hi_done"], C * (b + 1))
                    pe.wait_ge(s["x2_lo_done"], C * (b + 1))
                if k % (KF // 2) == 0:
                    ready = NFOLD * b + fold_at[("wi", 1, k // (KF // 2))] + 1
                    pe.wait_ge(s["w_hi_done"], ready)
                    pe.wait_ge(s["w_lo_done"], ready)
                need(pe, s["hid_lo_done"], KF * b + k - 1)
                for c in range(C):
                    cols = slice(k * P, (k + 1) * P)
                    mm = split_matmul(rb[k % 2][:, :], wi_hi[:, c, cols], wi_lo[:, c, cols], x2_hi[:, c, :], x2_lo[:, c, :],
                                      c == 0, c == C - 1)
                mm.then_inc(s["hid_mm"], 1)

            def output(b, k):
                if isinstance(b, int) and b == 0 and k == 0:
                    pe.wait_ge(s["srow_used"], 2)
                elif k == 0:
                    pe.wait_ge(s["x3_done"], b)
                if k % 2 == 0:
                    ready = NFOLD * b + fold_at[("wo", k // 2)] + 1
                    pe.wait_ge(s["w_hi_done"], ready)
                    pe.wait_ge(s["w_lo_done"], ready)
                pe.wait_ge(s["hid_hi_done"], KF * b + k + 1)
                pe.wait_ge(s["hid_lo_done"], KF * b + k + 1)
                for c in range(C):
                    cols = slice(c * P, (c + 1) * P)
                    mm = split_matmul(ob[:, c, :], wo_hi[:, k, cols], wo_lo[:, k, cols], hid_hi[:, k % 2, :],
                                      hid_lo[:, k % 2, :], k == 0, k == KF - 1)
                    if c == 0 and k == KF - 1 and isinstance(b, int) and b == B - 1:
                        mm.then_inc(s["end_out"], 1)
                mm.then_inc(s["out_mm"], 1)

            def keep_warm(count):
                for _ in range(count):
                    pe.matmul(ob[:, 0, :], zeros[:, 0:P], zeros[:, :], start=True, stop=True)

            pe.wait_ge(s["warm_zero"], 1)
            keep_warm(8)
            pe.wait_ge(s["ld_w1"], 32)
            project(0)
            project(1)
            score(0)
            score(1)
            pe.wait_ge(s["ld_cf"], 16)
            score_rows(0)
            project(2)
            project(3)
            score(2)
            score(3)
            spread_maxima(0)
            project(4)
            carry_sums(0)
            logits(0)
            project(5)
            score(4)
            pool_block(0, 0)
            pool_block(0, 1)
            score(5)
            pool_block(0, 2)
            pool_block(0, 3)
            project(6)
            for j in range(J):
                turn(0, j)
            project(7)
            score(6)
            fold(0, FOLDS[0])
            fold(0, FOLDS[1])
            layer1(0)
            fold(0, FOLDS[2])
            fold(0, FOLDS[3])
            score(7)
            keep_warm(3)
            score_rows(1)

            def step(b):
                n = b + 1
                hidden(b, 0)
                first = isinstance(b, int) and b == 0
                if first:
                    fold(0, FOLDS[4])
                    fold(0, FOLDS[5])
                hidden(b, 1)
                if not first:
                    fold(b, FOLDS[6])
                    fold(b, FOLDS[7])
                carry_sums(n)
                logits(n)
                output(b, 0)
                hidden(b, 2)
                if first:
                    fold(b, FOLDS[6])
                    fold(b, FOLDS[7])
                output(b, 1)
                hidden(b, 3)
                output(b, 2)
                fold(n, FOLDS[0])
                fold(n, FOLDS[1])
                hidden(b, 4)
                pool_block(n, 0)
                pool_block(n, 1)
                output(b, 3)
                fold(n, FOLDS[2])
                fold(n, FOLDS[3])
                pool_block(n, 2)
                hidden(b, 5)
                pool_block(n, 3)
                output(b, 4)
                hidden(b, 6)
                for j in range(J):
                    turn(n, j)
                output(b, 5)
                hidden(b, 7)
                layer1(n)
                fold(n, FOLDS[4])
                fold(n, FOLDS[5])
                output(b, 6)
                if first:
                    spread_maxima(1)
                output(b, 7)

            step(0)
            step(1)
            with pe.Fori(2, B - 1) as b:
                step(b)
            hidden(B - 1, 0)
            hidden(B - 1, 1)
            fold(B - 1, FOLDS[6])
            fold(B - 1, FOLDS[7])
            output(B - 1, 0)
            for k in range(2, KF):
                hidden(B - 1, k)
                output(B - 1, k - 1)
            output(B - 1, KF - 1)

        @block.scalar
        def _(act):
            def split_h(n):
                act.wait_ge(s["ld_xn"], 16 * (n + 1))
                need(act, s["num_mm"], J * n)
                act.activation(h_hi[:, :, 0:D], xn[:, ds(n & 1, 1)].rearrange("p o j d -> p (o j) d"),
                               ACT.Copy).then_inc(s["h_hi_done"], 1)

            def exps(n):
                act.wait_ge(s["logit_mm"], n + 1)
                need(act, s["p_lo_done"], n)
                for l in range(J):
                    act.activation(p_raw[:, 0, l * P:(l + 1) * P], xb[1][:, l * P:(l + 1) * P], ACT.Exp,
                                   bias=scol[group(n)][:, l, ds(n, 1)]).then_inc(s["exp_done"], 1)

            def round_carry(n):
                act.wait_ge(s["carry_mm"], n + 1)
                need(act, s["num_mm"], J * n)
                act.activation(cs[:, :], xb[0][:, 0:ND], ACT.Copy,
                               scale=cf[:, ds(n + CF_CSIGN, 1)]).then_inc(s["c_hi_done"], 1)

            def spread_exps(g):
                act.wait_ge(s["e_in_done"], g + 1)
                bs = GROUPS[g]
                act.activation(e_all[:, g, bs.start:bs.stop], e_in[:, g, bs.start:bs.stop], ACT.Exp).then_inc(s["e_done"], 1)
                act.activation(p_raw[:, 1, :], xb[0][:, :], ACT.Exp, bias=maxcol[:, g]).then_inc(s["coef_raw_done"], 1)

            def round_coef(g):
                act.wait_ge(s["coef_raw_done"], g + 1)
                act.activation(coef[g][:, :], p_raw[:, 1, :], ACT.Copy,
                               scale=cf[:, CF_SIGN + 2:CF_SIGN + 3]).then_inc(s["coef_hi_done"], 1)

            def start_pick(g):
                act.wait_ge(s["row_types"], 1)
                act.wait_ge(s["srow_step"], 2 * g + 1)
                if g:
                    act.wait_ge(s["m3_done"], g)
                act.activation(negmax[0:3 * Q, 0:S], rowbuf[g][0:3 * Q, 0, :], ACT.Copy,
                               scale=rowc[0:3 * Q, 0:1]).then_inc(s["pick_started"], 1)

            def place_mid(g):
                act.wait_ge(s["mid_done"], g + 1)
                act.activation(m3[g][Q:2 * Q, :], mid[Q:2 * Q, :], ACT.Copy).then_inc(s["mid_placed"], 1)

            def split_x1(n):
                act.wait_ge(s["turn_mm"], J * (n + 1))
                need(act, s["l1_mm"], C * n)
                act.activation(x1_hi[:, :, :], tb_[:, :, :], ACT.Copy).then_inc(s["x1_hi_done"], 1)

            def bias_x2(n):
                need(act, s["x3_done"], n - 1)
                for c in range(C):
                    act.wait_ge(s["l1_mm"], C * n + c + 1)
                    act.activation(x2[:, ds(n & 1, 1), c, :].rearrange("p o s -> p (o s)"), xb[c][:, :], ACT.Identity,
                                   bias=bc[:, ds(n & 1, 1), c]).then_inc(s["x2_done"], 1)

            def split_wc(n):
                act.wait_ge(s["wc_res_done"], 2 * (n + 1))
                need(act, s["l1_mm"], C * n)
                act.activation(wc_hi[:, :, :], wc_raw[:, :, :], ACT.Copy).then_inc(s["wc_hi_done"], 1)

            def round_lora(n, g):
                if g == 0:
                    act.wait_ge(s["ld_lora"], 2 * 16 * (n + 1))
                need(act, s["fold_mm"], NFOLD * n - 2 + 2 * g)
                for i, cols in enumerate(LORA[g]):
                    part, raw = ((la, la_raw), (lb, lb_raw))[i]
                    act.activation(part[:, cols], raw[:, cols], ACT.Copy,
                                   scale=cf[:, CF_SIGN + i:CF_SIGN + i + 1]).then_inc(s["lora_hi_done"], 1)

            def relu_hidden(b, k):
                act.wait_ge(s["hid_mm"], KF * b + k + 1)
                need(act, s["out_mm"], KF * b + k - 1)
                act.activation(hid_hi[:, k % 2, :], rb[k % 2][:, :], ACT.Relu).then_inc(s["hid_hi_done"], 1)

            def split_w(n, i):
                act.wait_ge(s["w_sum_done"], NFOLD * n + i + 1)
                used = KF * n - (KF // 2 if i < NFOLD // 2 else 0)
                need(act, s["hid_mm"] if FOLDS[i][0] == "wi" else s["out_mm"], used)
                act.activation(wfold(FOLDS[i], "hi"), w_sum[:, i % WS, :], ACT.Copy).then_inc(s["w_hi_done"], 1)

            def linear(b):
                act.wait_ge(s["x3_done"], b + 1)
                need(act, s["quad_done"], b)
                if isinstance(b, int) and b == 0:
                    act.wait_ge(s["m3_done"], 2)
                act.activation(t_lin, x3[:, :, :], ACT.Identity, bias=zc[:, 1, ds(b, 1)],
                               scale=zc[:, 2, ds(b, 1)]).then_inc(s["lin_done"], 1)

            def tanh(b):
                act.wait_ge(s["proj_mm"], b + 1)
                if b >= 2:
                    act.wait_ge(s["score_mm"], b - 1)
                act.activation(tanhT[:, b % 2, :], rb[b % 2][0:A, :], ACT.Tanh, bias=b1v[:, 0:1]).then_inc(s["tanh_done"], 1)

            act.wait_ge(s["warm_zero"], 1)
            act.activation(tanh_warm[:, :], zeros[:, 0:1], ACT.Tanh)
            act.wait_ge(s["ld_w1"], 32)
            tanh(0)
            tanh(1)
            split_h(0)
            act.wait_ge(s["ld_cf"], 16)
            start_pick(0)
            tanh(2)
            tanh(3)
            act.wait_ge(s["ld_common"], 2 * 16)
            round_lora(0, 0)
            spread_exps(0)
            tanh(4)
            place_mid(0)
            round_coef(0)
            round_carry(0)
            exps(0)
            tanh(5)
            round_lora(0, 1)
            split_wc(0)
            tanh(6)
            split_x1(0)
            tanh(7)
            split_h(1)
            split_w(0, 0)
            split_w(0, 1)
            bias_x2(0)
            split_w(0, 2)
            split_w(0, 3)

            def step(b, last=False, h_left=True):
                n = b + 1
                first = isinstance(b, int) and b == 0
                relu_hidden(b, 0)
                if first:
                    start_pick(1)
                    split_w(b, 4)
                    split_w(b, 5)
                relu_hidden(b, 1)
                if isinstance(b, int) and b == 1:
                    round_coef(1)
                if not first:
                    linear(b - 1)
                    split_w(b, 6)
                    split_w(b, 7)
                if last:
                    for k in range(2, KF):
                        relu_hidden(b, k)
                    return
                round_carry(n)
                exps(n)
                relu_hidden(b, 2)
                round_lora(n, 0)
                if first:
                    split_w(b, 6)
                    split_w(b, 7)
                relu_hidden(b, 3)
                round_lora(n, 1)
                relu_hidden(b, 4)
                split_w(n, 0)
                split_w(n, 1)
                split_wc(n)
                relu_hidden(b, 5)
                split_w(n, 2)
                split_w(n, 3)
                relu_hidden(b, 6)
                split_x1(n)
                if h_left:
                    split_h(n + 1)
                relu_hidden(b, 7)
                if first:
                    place_mid(1)
                bias_x2(n)
                split_w(n, 4)
                split_w(n, 5)
                if first:
                    spread_exps(1)

            step(0)
            step(1)
            with act.Fori(2, B - 2) as b:
                step(b)
            step(B - 2, h_left=False)
            step(B - 1, last=True)
            act.wait_ge(s["quad_done"], B - 1)
            for c in range(C):
                act.wait_ge(s["end_x3"], c + 1)
                act.activation(t_lin[:, c, :], x3[:, c, :], ACT.Identity, bias=zc[:, 1, B - 1:B],
                               scale=zc[:, 2, B - 1:B]).then_inc(s["end_lin"], 1)

        @block.vector
        def _(v):
            steps = [0]

            def link(ins):
                ins.then_inc(s["dve_step"], 1)
                steps[0] += 1
                v.wait_ge(s["dve_step"], steps[0])

            def scores_in(b):
                g = group(b)
                v.wait_ge(s["score_mm"], b + 1)
                src = rb[b % 2][:, 0:J].rearrange("p (j o) -> p j o", o=1).broadcast_to([P, J, 3])
                v.tensor_copy(scol[g][:, :, b:b + 2 * Q + 1:Q], src).then_inc(s["scol_done"], 1)

            def types_masks():
                v.wait_ge(s["ld_types"], 32)
                link(v.tensor_copy(types[:, :], types_i[:, :]))
                for col in range(2):
                    link(v.tensor_scalar(batc[:, col], types[:, :], float(col), None, ALU.is_equal))
                link(v.tensor_tensor(batc[:, 3], batc[:, 0], batc[:, 1], ALU.add))
                link(v.tensor_scalar(batc[:, 2], batc[:, 3], -1.0, 1.0, ALU.mult, ALU.add))
                v.tensor_scalar(batneg[:, :, :], batc[:, 0:3], NEG, None, ALU.mult).then_inc(s["types_done"], 1)
                link(v.tensor_copy(typeq[:, :], typeq_i[:, :]))
                for col in range(2):
                    link(v.tensor_scalar(rowc[:, col:col + 1], typeq[:, :], float(col), None, ALU.is_equal))
                link(v.tensor_tensor(rowc[:, 3:4], rowc[:, 0:1], rowc[:, 1:2], ALU.add))
                link(v.tensor_scalar(rowc[:, 2:3], rowc[:, 3:4], -1.0, 1.0, ALU.mult, ALU.add))
                link(v.tensor_scalar(rowneg[:, :], rowc[:, 0:3], NEG, None, ALU.mult))
                v.tensor_scalar(rowc[:, 0:3], rowc[:, 0:3], -1.0, None, ALU.mult).then_inc(s["row_types"], 1)
                v.wait_ge(s["row_types"], 1)
                v.wait_ge(s["ld_cb"], 16)
                link(v.tensor_scalar(blockneg[:, :], cb[:, CB_MASK:CB_MASK + J], rowneg[:, 0:1], None, ALU.mult))
                for t in (1, 2):
                    link(v.scalar_tensor_tensor(out=blockneg[:, :], in0=cb[:, CB_MASK + t * J:CB_MASK + (t + 1) * J],
                                                scalar=rowneg[:, t:t + 1], in1=blockneg[:, :], op0=ALU.mult, op1=ALU.add))
                q3 = slice(3 * Q, 4 * Q)
                for tile in (m3[0], m3[1], negmax):
                    link(v.tensor_copy(tile[q3, 0:S].rearrange("p (j t) -> p j t", j=J),
                                       blockneg[q3, :].rearrange("p (j o) -> p j o", o=1).broadcast_to([Q, J, P])))
                    link(v.memset(tile[q3, S:S + J], 0.0))

            def counts():
                v.wait_ge(s["ld_cf"], 16)
                link(v.tensor_tensor(cnt_a[:, :], batc[:, 0], batc[:, 1], ALU.subtract))
                link(v.tensor_scalar(cnt_b[:, :], batc[:, 1], float(S + 1), None, ALU.mult))
                link(v.scalar_tensor_tensor(out=cnt_b[:, :], in0=batc[:, 2], scalar=float(S - 1), in1=cnt_b[:, :],
                                            op0=ALU.mult, op1=ALU.add))
                for j in range(J):
                    link(v.scalar_tensor_tensor(out=cnt[:, :, j], in0=cnt_a[:, :], scalar=cf[:, CF_TOK + j:CF_TOK + j + 1],
                                                in1=cnt_b[:, :], op0=ALU.mult, op1=ALU.add))

            def reaction():
                v.wait_ge(s["ld_z"], 16)
                link(v.tensor_tensor(zc[:, 0], z[:, 0], z[:, 1], ALU.add))
                link(v.tensor_scalar(zc[:, 1], zc[:, 0], -2.0, 1.0, ALU.mult, ALU.add))
                link(v.tensor_tensor(zc[:, 1], zc[:, 1], z[:, 2], ALU.add))
                link(v.tensor_scalar(zc[:, 2], z[:, 2], -1.0, None, ALU.mult))

            rows = slice(0, 3 * Q)

            def row_maxima(g):
                premax, postmax = (rowbuf[g][rows, i, :] for i in range(2))
                srow = score_bank(g)[rows, :]
                floor = lowest[rows, :].broadcast_to([3 * Q, S])
                v.wait_ge(s["turned"], g + 1)
                v.tensor_tensor_scan(premax, srow, floor, -3e38, ALU.max, ALU.max).then_inc(s["srow_step"], 1)
                v.tensor_tensor_scan(postmax[:, ::-1], srow[:, ::-1], floor, -3e38, ALU.max, ALU.max)\
                    .then_inc(s["srow_step"], 1)
                v.tensor_reduce(blockmax[rows, g, :], srow.rearrange("p (j t) -> p j t", j=J), mybir.AxisListType.X,
                                ALU.max).then_inc(s["srow_used"], 1)
                v.wait_ge(s["srow_used"], g + 1)
                link(v.tensor_scalar(negmax[rows, S:S + J], blockmax[rows, g, :], -1.0, None, ALU.mult))

            def others_maxima(g):
                premax, postmax, exmax = (rowbuf[g][rows, i, :] for i in range(3))
                v.wait_ge(s["srow_step"], 2 * (g + 1))
                link(v.tensor_tensor(exmax[:, 1:S - 1], premax[:, 0:S - 2], postmax[:, 2:S], ALU.max))
                link(v.tensor_copy(exmax[:, 0:1], postmax[:, 1:2]))
                link(v.tensor_copy(exmax[:, S - 1:S], premax[:, S - 2:S - 1]))

            def pick_maxima(g):
                premax, postmax, exmax = (rowbuf[g][rows, i, :] for i in range(3))
                out = negmax[rows, 0:S]
                v.wait_ge(s["pick_started"], g + 1)
                link(v.scalar_tensor_tensor(out=out, in0=postmax, scalar=rowc[rows, 1:2], in1=out, op0=ALU.mult, op1=ALU.add))
                v.scalar_tensor_tensor(out=out, in0=exmax, scalar=rowc[rows, 2:3], in1=out, op0=ALU.mult, op1=ALU.add)\
                    .then_inc(s["negmax_done"], 1)

            def part_high(g):
                v.wait_ge(s["negmax_done"], g + 1)
                link(v.tensor_copy(m3[g][rows, :], negmax[rows, :]))
                link(v.tensor_tensor(rest[:, :], negmax[rows, :], m3[g][rows, :], ALU.subtract))

            def part_rest(g):
                v.tensor_copy(mid[:, :], rest[:, :]).then_inc(s["mid_done"], 1)
                v.wait_ge(s["mid_done"], g + 1)
                link(v.tensor_tensor(rest[:, :], rest[:, :], mid[:, :], ALU.subtract))
                v.tensor_copy(m3[g][2 * Q:3 * Q, :], rest[2 * Q:3 * Q, :]).then_inc(s["m3_done"], 1)

            def spread_in(g):
                bs = GROUPS[g]
                v.wait_ge(s["spread_mm"], g + 1)
                link(v.tensor_tensor(maxtmp[:, :], xb[1][:, B * J:(B + 1) * J], cf[:, CF_PICK:CF_PICK + J], ALU.mult))
                link(v.tensor_reduce(maxcol[:, g], maxtmp[:, :], mybir.AxisListType.X, ALU.add))
                v.tensor_tensor(e_in[:, g, bs.start:bs.stop], xb[1][:, bs.start * J:bs.stop * J].rearrange("p (b j) -> p b j", j=J),
                                scol[g][:, :, bs.start:bs.stop].rearrange("p j b -> p b j"), ALU.add).then_inc(s["e_in_done"], 1)

            def split_coef(g):
                v.wait_ge(s["coef_hi_done"], g + 1)
                v.scalar_tensor_tensor(out=coef[g][:, :], in0=p_raw[:, 1, :], scalar=cf[:, CF_LO + 2:CF_LO + 3],
                                       in1=coef[g][:, :].bitcast(F32), op0=ALU.mult, op1=ALU.add).then_inc(s["coef_done"], 1)

            def spread_e(n):
                if isinstance(n, int) and n in (0, 2):
                    v.wait_ge(s["e_done"], group(n) + 1)
                    v.wait_ge(s["e4_zero"], 2)
                need(v, s["carry_mm"], n)
                e = e_all[:, group(n), ds(n, 1), :].rearrange("p o j -> p (o j)").rearrange("p (j o) -> p j o", o=1)\
                    .broadcast_to([P, J, Q])
                v.tensor_scalar(spread(e4_hi), e, 1.0, None, ALU.mult).then_inc(s["e4_hi_done"], 1)
                v.wait_ge(s["e4_hi_done"], n + 1)
                v.tensor_tensor(spread(e4_lo), e, spread(e4_hi).bitcast(F32), ALU.subtract).then_inc(s["e4_lo_done"], 1)

            def split_carry(n):
                v.wait_ge(s["c_hi_done"], n + 1)
                v.scalar_tensor_tensor(out=cs[:, :], in0=xb[0][:, 0:ND], scalar=cf[:, ds(n + CF_CLO, 1)],
                                       in1=cs[:, :].bitcast(F32), op0=ALU.mult, op1=ALU.add).then_inc(s["c_done"], 1)

            def split_p(n):
                v.wait_ge(s["exp_done"], J * (n + 1))
                need(v, s["num_mm"], J * n)
                v.tensor_copy(p_hi[:, :], p_raw[:, 0, :]).then_inc(s["p_hi_done"], 1)
                v.wait_ge(s["p_hi_done"], n + 1)
                v.tensor_tensor(p_lo[:, :], p_raw[:, 0, :], p_hi[:, :].bitcast(F32), ALU.subtract).then_inc(s["p_lo_done"], 1)

            def finish_x1(n, j):
                v.wait_ge(s["num_mm"], J * n + j + 1)
                v.tensor_tensor(den[:, 0, j:j + 1], xb[j % 2][:, D:D + 1], cnt[:, ds(n, 1), j], ALU.mult).then_inc(s["den_step"], 1)
                v.wait_ge(s["den_step"], 2 * (J * n + j) + 1)
                v.reciprocal(den[:, 1, j:j + 1], den[:, 0, j:j + 1]).then_inc(s["den_step"], 1)
                v.wait_ge(s["den_step"], 2 * (J * n + j) + 2)
                need(v, s["turn_mm"], J * (n - 1) + j + 1)
                v.scalar_tensor_tensor(out=x1n[:, j, :], in0=xb[j % 2][:, 0:D], scalar=den[:, 1, j:j + 1],
                                       in1=xn[:, ds(n & 1, 1), j, :].rearrange("p o d -> p (o d)"), op0=ALU.mult,
                                       op1=ALU.add).then_inc(s["x1_done"], 1)

            def split_lora(n, g):
                for i, cols in enumerate(LORA[g]):
                    part, raw = ((la, la_raw), (lb, lb_raw))[i]
                    v.wait_ge(s["lora_hi_done"], 4 * n + 2 * g + i + 1)
                    v.scalar_tensor_tensor(out=part[:, cols], in0=raw[:, cols], scalar=cf[:, CF_LO + i:CF_LO + i + 1],
                                           in1=part[:, cols].bitcast(F32), op0=ALU.mult, op1=ALU.add).then_inc(s["lora_done"], 1)

            def split_x1(n):
                v.wait_ge(s["x1_hi_done"], n + 1)
                need(v, s["l1_mm"], C * n)
                v.tensor_tensor(x1_lo[:, :, :], tb_[:, :, :], x1_hi[:, :, :].bitcast(F32), ALU.subtract).then_inc(s["x1_lo_done"], 1)

            def split_x2(n, chunks=range(C)):
                need(v, s["hid_mm"], KF * n)
                for c in chunks:
                    x2_c = x2[:, ds(n & 1, 1), c, :].rearrange("p o s -> p (o s)")
                    v.wait_ge(s["x2_done"], C * n + c + 1)
                    v.tensor_scalar(x2_hi[:, c, :], x2_c, 1.0, None, ALU.mult).then_inc(s["x2_hi_done"], 1)
                    v.wait_ge(s["x2_hi_done"], C * n + c + 1)
                    v.tensor_tensor(x2_lo[:, c, :], x2_c, x2_hi[:, c, :].bitcast(F32), ALU.subtract).then_inc(s["x2_lo_done"], 1)

            def add_w(n, i):
                v.wait_ge(s["fold_mm"], NFOLD * n + i + 1)
                need(v, s["w_hi_done"], NFOLD * n + i - WS + 1)
                need(v, s["w_lo_done"], NFOLD * n + i - WS + 1)
                v.scalar_tensor_tensor(out=w_sum[:, i % WS, :], in0=tb_[:, i % 2, :], scalar=LORA_ALPHA,
                                       in1=wfold(FOLDS[i], "raw"), op0=ALU.mult, op1=ALU.add).then_inc(s["w_sum_done"], 1)

            def split_hidden(b, k):
                v.wait_ge(s["hid_hi_done"], KF * b + k + 1)
                need(v, s["out_mm"], KF * b + k - 1)
                v.scalar_tensor_tensor(out=hid_lo[:, k % 2, :], in0=rb[k % 2][:, :], scalar=0.0, in1=hid_hi[:, k % 2, :].bitcast(F32),
                                       op0=ALU.max, op1=ALU.subtract).then_inc(s["hid_lo_done"], 1)

            def finish_x3(b):
                v.wait_ge(s["out_mm"], KF * (b + 1))
                need(v, s["lin_done"], b)
                need(v, s["y_done"], 3 * b)
                need(v, s["prod_done"], b)
                need(v, s["near_done"], C * b)
                need(v, s["quad_done"], b)
                v.tensor_tensor(x3[:, :, :], ob[:, :, :], x2[:, ds(b & 1, 1)].rearrange("p o c s -> p (o c) s"),
                                ALU.add).then_inc(s["x3_done"], 1)

            def quadratic(b):
                v.wait_ge(s["prod_done"], b + 1)
                v.wait_ge(s["near_done"], C * (b + 1))
                need(v, s["out_done"], b)
                v.scalar_tensor_tensor(out=t_quad, in0=x3_next[:, :, :], scalar=z[:, 0, ds(b, 1)], in1=t_lin, op0=ALU.mult,
                                       op1=ALU.add).then_inc(s["quad_done"], 1)

            def finish_out(b):
                v.wait_ge(s["y_done"], 3 * (b + 1))
                v.wait_ge(s["quad_done"], b + 1)
                need(v, s["stored"], 16 * b)
                v.scalar_tensor_tensor(out=t_out, in0=t_y, scalar=z[:, 1, ds(b, 1)], in1=t_quad, op0=ALU.mult,
                                       op1=ALU.add).then_inc(s["out_done"], 1)

            def finish_last():
                b, z_x, z_y = B - 1, z[:, 0, B - 1:B], z[:, 1, B - 1:B]
                v.wait_ge(s["lin_done"], b)
                v.wait_ge(s["y_done"], 3 * b)
                v.wait_ge(s["prod_done"], b)
                v.wait_ge(s["near_done"], C * b)
                v.wait_ge(s["quad_done"], b)
                for c in range(C):
                    v.wait_ge(*((s["end_out"], 1) if c == 0 else (s["out_mm"], KF * B)))
                    v.tensor_tensor(x3[:, c, :], ob[:, c, :], x2[:, b % 2, c, :], ALU.add).then_inc(s["end_x3"], 1)
                v.wait_ge(s["out_done"], b)
                v.wait_ge(s["end_x3"], C)
                for c in range(C):
                    v.wait_ge(s["end_lin"], c + 1)
                    link(v.tensor_tensor(t_lin[:, c, :], t_lin[:, c, :], x3[:, c, :], ALU.mult))
                    link(v.scalar_tensor_tensor(out=t_quad[:, c, :], in0=x3[:, 1 - c, :], scalar=z_x, in1=t_lin[:, c, :],
                                                op0=ALU.mult, op1=ALU.add))
                v.wait_ge(s["stored"], 16 * b)
                for c in (1, 0):
                    v.wait_ge(s["end_y"], 3 * (c + 1))
                    link(v.scalar_tensor_tensor(out=t_quad[:, c, :], in0=t_y[:, c, :], scalar=z_y, in1=t_quad[:, c, :],
                                                op0=ALU.mult, op1=ALU.add))
                    v.wait_ge(end_shifted[c], 2 * 16)
                    v.scalar_tensor_tensor(out=t_out[:, c, :], in0=x3_next[:, c, :], scalar=z_x, in1=t_quad[:, c, :],
                                           op0=ALU.mult, op1=ALU.add).then_inc(s["out_done"], 1)

            v.memset(zeros[:, :], 0.0).then_inc(s["warm_zero"], 1)
            v.memset(scol[0][:, :, :], 0.0).then_inc(s["zeros_done"], 1)
            v.memset(scol[1][:, :, :], 0.0).then_inc(s["zeros_done"], 1)
            v.memset(lowest[:, :], -3e38).then_inc(s["zeros_done"], 1)
            types_masks()
            counts()
            v.wait_ge(s["zeros_done"], 3)
            scores_in(0)
            scores_in(1)
            row_maxima(0)
            others_maxima(0)
            pick_maxima(0)
            scores_in(2)
            scores_in(3)
            part_high(0)
            spread_in(0)
            spread_e(0)
            part_rest(0)
            split_coef(0)
            split_carry(0)
            split_p(0)
            scores_in(4)
            finish_x1(0, 0)
            finish_x1(0, 1)
            scores_in(5)
            split_lora(0, 0)
            finish_x1(0, 2)
            finish_x1(0, 3)
            split_lora(0, 1)
            split_x1(0)
            scores_in(6)
            v.wait_ge(s["ld_wi"], 16)
            add_w(0, 0)
            add_w(0, 1)
            reaction()
            split_x2(0, (0,))
            split_x2(0, (1,))
            scores_in(7)
            v.wait_ge(s["ld_wo"], 16)
            add_w(0, 2)
            add_w(0, 3)
            spread_e(1)
            row_maxima(1)

            def step(b, last=False, e_left=True):
                n = b + 1
                first = isinstance(b, int) and b == 0
                split_hidden(b, 0)
                if first:
                    add_w(b, 4)
                    add_w(b, 5)
                    others_maxima(1)
                split_hidden(b, 1)
                if not first:
                    add_w(b, 6)
                    add_w(b, 7)
                if last:
                    for k in range(2, KF):
                        split_hidden(b, k)
                        if k == KF - 3:
                            quadratic(b - 1)
                        if k == KF - 2:
                            finish_out(b - 1)
                    return
                if isinstance(b, int) and b == 1:
                    split_coef(1)
                split_carry(n)
                split_p(n)
                split_hidden(b, 2)
                if first:
                    add_w(b, 6)
                    add_w(b, 7)
                split_lora(n, 0)
                split_hidden(b, 3)
                split_lora(n, 1)
                add_w(n, 0)
                add_w(n, 1)
                finish_x1(n, 0)
                split_hidden(b, 4)
                finish_x1(n, 1)
                add_w(n, 2)
                add_w(n, 3)
                finish_x1(n, 2)
                finish_x1(n, 3)
                split_hidden(b, 5)
                if first:
                    pick_maxima(1)
                else:
                    quadratic(b - 1)
                split_hidden(b, 6)
                split_x1(n)
                if first:
                    part_high(1)
                    part_rest(1)
                split_hidden(b, 7)
                if not first:
                    finish_out(b - 1)
                split_x2(n)
                add_w(n, 4)
                add_w(n, 5)
                if first:
                    spread_in(1)
                if e_left:
                    spread_e(n + 1)
                finish_x3(b)

            step(0)
            step(1)
            with v.Fori(2, B - 2) as b:
                step(b)
            step(B - 2, e_left=False)
            step(B - 1, last=True)
            finish_last()

        @block.gpsimd
        def _(pool):
            def add_residual(n):
                pool.wait_ge(s["ld_wc"], 32 * (n + 1))
                for c in range(C):
                    diag = wc_raw[:, c, c * P:(c + 1) * P]
                    pool.tensor_tensor(diag, diag, cf[:, CF_ID:CF_ID + P], ALU.add).then_inc(s["wc_res_done"], 1)

            def split_wc(n):
                pool.wait_ge(s["wc_hi_done"], n + 1)
                need(pool, s["l1_mm"], C * n)
                pool.tensor_tensor(wc_lo[:, :, :], wc_raw[:, :, :], wc_hi[:, :, :].bitcast(F32), ALU.subtract).then_inc(s["wc_lo_done"], 1)

            def split_w(n, i):
                pool.wait_ge(s["w_hi_done"], NFOLD * n + i + 1)
                pool.tensor_tensor(wfold(FOLDS[i], "lo"), w_sum[:, i % WS, :], wfold(FOLDS[i], "hi").bitcast(F32),
                                   ALU.subtract).then_inc(s["w_lo_done"], 1)

            def along_tokens(b):
                pool.wait_ge(s["x3_done"], b + 1)
                need(pool, s["out_done"], b)
                ends = ((0, 1), (S - 1, S - 2))
                for t, at in ends:
                    pool.tensor_tensor(t_y[:, :, t:t + 1], x3[:, :, at:at + 1], x3[:, :, at:at + 1],
                                       ALU.add).then_inc(s["y_done"], 1)
                pool.tensor_tensor(t_y[:, :, 1:S - 1], x3[:, :, 0:S - 2], x3[:, :, 2:S], ALU.add).then_inc(s["y_done"], 1)

            def split_h(n):
                pool.wait_ge(s["h_hi_done"], n + 1)
                need(pool, s["num_mm"], J * n)
                pool.tensor_tensor(h_lo[:, :, 0:D], xn[:, ds(n & 1, 1)].rearrange("p o j d -> p (o j) d"),
                                   h_hi[:, :, 0:D].bitcast(F32), ALU.subtract).then_inc(s["h_lo_done"], 1)

            def selectors(g):
                bs = GROUPS[g]
                pool.tensor_copy(sel[:, bs.start:bs.stop, :],
                                 cb[:, CB_HOT + bs.start:CB_HOT + bs.stop].rearrange("p (k o) -> p k o", o=1)
                                 .broadcast_to([P, len(bs), P])).then_inc(s["sel_done"], 1)

            def diagonal_masks(g):
                bs = slice(GROUPS[g].start, GROUPS[g].stop)
                shape = [P, len(GROUPS[g]), P]
                pool.wait_ge(s["types_done"], 1)
                mask, *terms = diagmask[:, bs, :], diagterm[:, 0, bs, :], diagterm[:, 1, bs, :]
                for t, (col, to) in enumerate(zip((CB_LO, CB_UP, CB_ID), (mask, *terms))):
                    pool.tensor_tensor(to, cb[:, col:col + P].rearrange("p (o m) -> p o m", o=1).broadcast_to(shape),
                                       batneg[:, t, bs].rearrange("p (b o) -> p b o", o=1).broadcast_to(shape),
                                       ALU.mult).then_inc(s["diag_step"], 1)
                pool.wait_ge(s["diag_step"], 4 * g + 3)
                pool.tensor_tensor(mask, mask, terms[0], ALU.add).then_inc(s["diag_step"], 1)
                pool.wait_ge(s["diag_step"], 4 * g + 4)
                pool.tensor_tensor(mask, mask, terms[1], ALU.add).then_inc(s["diag_done"], 1)

            pool.memset(h_lo[:, :, D:ND].bitcast(F32), 0.0).then_inc(s["ones_done"], 1)
            pool.memset(h_hi[:, :, D:ND].bitcast(F32), 1.0).then_inc(s["ones_done"], 1)
            pool.memset(e4_hi[:, :].bitcast(F32), 0.0).then_inc(s["e4_zero"], 1)
            pool.memset(e4_lo[:, :].bitcast(F32), 0.0).then_inc(s["e4_zero"], 1)
            pool.memset(sel_f[:, :, :], 0.0).then_inc(s["sel_f_done"], 1)
            pool.wait_ge(s["ld_cb"], 16)
            pool.wait_ge(s["sel_f_done"], 1)
            pool.tensor_copy(sel_f[0:Q, 0:2, :], cb[0:Q, CB_HOT:CB_HOT + 2].rearrange("p (k o) -> p k o", o=1)
                             .broadcast_to([Q, 2, P])).then_inc(s["sel_f_done"], 1)
            for i, quadrant in enumerate((slice(0, Q), slice(3 * Q, P))):
                pool.wait_ge(s["sel_f_done"], 2 + i)
                pool.tensor_copy(sel_f[quadrant, 2, :], cb[quadrant, CB_CSEL:CB_CSEL + P]).then_inc(s["sel_f_done"], 1)
            pool.wait_ge(s["sel_f_done"], 4)
            selectors(0)
            diagonal_masks(0)
            split_h(0)
            selectors(1)
            diagonal_masks(1)
            pool.wait_ge(s["ld_cf"], 16)
            add_residual(0)
            split_wc(0)
            split_w(0, 0)
            split_w(0, 1)
            split_h(1)
            for i in range(2, EARLY):
                split_w(0, i)

            def step(b, last=False, h_left=True):
                n = b + 1
                for i in range(EARLY, NFOLD):
                    split_w(b, i)
                if not (isinstance(b, int) and b == 0):
                    product(pool, b - 1)
                    along_tokens(b - 1)
                if not last:
                    add_residual(n)
                if not (isinstance(b, int) and b == 0):
                    near_features(pool, b - 1)
                if last:
                    return
                split_w(n, 0)
                split_w(n, 1)
                split_wc(n)
                split_w(n, 2)
                split_w(n, 3)
                if h_left:
                    split_h(n + 1)
                for i in range(NFOLD // 2, EARLY):
                    split_w(n, i)

            step(0)
            step(1)
            with pool.Fori(2, B - 2) as b:
                step(b)
            step(B - 2, h_left=False)
            step(B - 1, last=True)
            pool.wait_ge(s["out_done"], B - 1)
            for c in range(C):
                pool.wait_ge(s["end_x3"], c + 1)
                for to, before, behind in ((slice(1, S - 1), slice(0, S - 2), slice(2, S)), (slice(0, 1), slice(1, 2), slice(1, 2)),
                                           (slice(S - 1, S), slice(S - 2, S - 1), slice(S - 2, S - 1))):
                    pool.tensor_tensor(t_y[:, c, to], x3[:, c, before], x3[:, c, behind], ALU.add).then_inc(s["end_y"], 1)


def kernel(**inputs):
    import ml_dtypes
    import numpy as np

    import concourse.bacc as bacc
    from concourse.bass_utils import run_bass_kernel_spmd

    a = {k: np.asarray(v) for k, v in inputs.items()}
    bf16 = ml_dtypes.bfloat16

    def halves(x, axis):
        x = np.moveaxis(x, axis, -1)
        x = np.moveaxis(x.reshape(x.shape[:-1] + (P, C)), -1, -2)
        return np.moveaxis(x, (-2, -1), (axis, axis + 1))

    p, m = np.arange(P)[:, None], np.arange(P)[None, :]
    cf = np.zeros((P, CF_N), np.float32)
    cf[:, CF_ID:CF_ID + P] = p == m
    cf[:, CF_TOK:CF_TOK + J] = np.arange(J)[None, :] * P + p + 1
    copy = p // RC % 4
    for i, low in enumerate((copy % 2 == 1, copy >= 2, p // Q >= 2)):
        cf[:, CF_LO + i:CF_LO + i + 1] = low
        cf[:, CF_SIGN + i:CF_SIGN + i + 1] = 1 - 2 * low
    cb = np.zeros((P, CB_N), np.float32)
    cb[:, CB_ID:CB_ID + P] = p == m
    cb[:, CB_LO:CB_LO + P] = p > m
    cb[:, CB_UP:CB_UP + P] = p < m
    blk = np.arange(J)
    for b in range(B):
        cb[[b, Q + b, 2 * Q + b], CB_HOT + b] = 1
        for l in range(J):
            row = 3 * Q + b * J + l
            for t, masked in enumerate((l >= blk, l <= blk, l == blk)):
                cb[row, CB_MASK + t * J:CB_MASK + (t + 1) * J] = masked
            for q in range(4):
                cb[[b, Q + b, 2 * Q + b, row], CB_CSEL + q * Q + b * J + l] = 1
    for b in range(B):
        own = p % Q // J == b
        cf[:, CF_CLO + b:CF_CLO + b + 1] = own * (p // Q % 2 == 1)
        cf[:, CF_CSIGN + b:CF_CSIGN + b + 1] = own * (1 - 2 * (p // Q % 2 == 1))
    cf[:, CF_PICK:CF_PICK + J] = -1.0 * (p % J == np.arange(J)[None, :])
    types = a["itok_B_0_2"]
    typeq = np.zeros((P, 1), types.dtype)
    for q in range(3):
        typeq[q * Q:q * Q + B, 0] = types
    typeq[3 * Q:, 0] = np.repeat(types, J)
    x = a["x"]
    wc = halves(a["L1_cond_W"].reshape(-1, P, C, D), 3)
    arrays = {
        "xT": x.transpose(0, 2, 1).reshape(B, P, C, S),
        "xn": halves(x, 2).reshape(B, J, P, D).transpose(0, 2, 1, 3),
        "cf": cf,
        "cb": cb.astype(bf16),
        "typeq": typeq,
        "types": np.broadcast_to(types, (P, B)),
        "ids": np.concatenate([a["itok_B_0_30"], a["itok_B_0_7"]])[None, :],
        "z": np.broadcast_to(np.stack([a["condB_zX"], a["condB_zY"], a["condB_zR"]]), (P, 3, B)),
        "w1": a["L0_cond_W1"].reshape(P, C, A),
        "b1v": np.stack([a["L0_cond_b1"], a["L0_cond_v"]], axis=1),
        "wc": wc.reshape(-1, P, C, D),
        "bc": a["L1_cond_b"].reshape(-1, P, C),
        "wi": a["L2_cond_wi"].T.reshape(P, C, F),
        "wo": halves(a["L2_cond_wo"].T, 1).reshape(KF, P, D).transpose(1, 0, 2),
        "la_common": np.concatenate([halves(a["L2_cond_common_wi_a"], 1).reshape(-1, D), a["L2_cond_common_wo_a"]], axis=1),
        "la_expert": np.concatenate([halves(a["L2_cond_experts_wi_a"], 2).reshape(NEXP, -1, D), a["L2_cond_experts_wo_a"]], axis=2),
        "lb_common": np.concatenate([a["L2_cond_common_wi_b"].T, halves(a["L2_cond_common_wo_b"].T, 1).reshape(-1, D)], axis=1),
        "lb_expert": np.concatenate([a["L2_cond_experts_wi_b"].transpose(0, 2, 1),
                                     halves(a["L2_cond_experts_wo_b"].transpose(0, 2, 1), 2).reshape(NEXP, -1, D)], axis=2),
    }
    for name in ("la_common", "lb_common"):
        arrays[name] = np.tile(arrays[name], (4, 1))
    for name in ("la_expert", "lb_expert"):
        arrays[name] = np.tile(arrays[name], (1, 4, 1))
    nc = bacc.Bacc("TRN2", target_bir_lowering=False, num_devices=1)
    feed, args = {}, []
    for name, array in arrays.items():
        array = np.ascontiguousarray(array)
        feed[f"{name}_dram"] = array
        args.append(nc.dram_tensor(f"{name}_dram", array.shape, mybir.dt.from_np(array.dtype), kind="ExternalInput").ap())
    out = nc.dram_tensor("out_dram", (B, P, C, S), F32, kind="ExternalOutput").ap()
    build(nc, *args, out)
    got = run_bass_kernel_spmd(nc, [feed], core_ids=[0]).results[0]["out_dram"]
    return np.ascontiguousarray(np.asarray(got).reshape(B, D, S).transpose(0, 2, 1))
```
